# Optimizing a Trainium2 kernel written in Bass

```python
import numpy as np
import jax
import jax.numpy as jnp

def _softmax(x, axis=-1):
    return jax.nn.softmax(x, axis=axis)

def _gelu(x):
    return jax.nn.gelu(x, approximate=True)

def _silu(x):
    return jax.nn.silu(x)

def _sigmoid(x):
    return jax.nn.sigmoid(x)

def _layernorm(x, axis=-1, eps=1e-05):
    m = jnp.mean(x, axis=axis, keepdims=True)
    v = jnp.var(x, axis=axis, keepdims=True)
    return (x - m) / jnp.sqrt(v + eps)

def _scatter_add(tgt, idx, src, axis=0):
    return tgt.at[idx].add(src)

def _segment_sum(src, seg, n):
    return jax.ops.segment_sum(src, seg, n)
kernel_name = 'mk_flamingo_gated_d2_seqx_r8_983418'

def setup_inputs(seed: int=0):
    np.random.seed(seed)
    _w = jnp.asarray

    def _rec_inputs():
        import jax
        import jax.numpy as jnp
        _rk = jax.random.key(seed)
        x = -0.0003929 + 0.9999 * jax.random.normal(jax.random.fold_in(_rk, 1), (32, 100, 128), jnp.float32)
        _lenS = 100 - jax.random.randint(jax.random.fold_in(_rk, 7), (32,), 0, max(1, 100 // 4) + 1, jnp.int32)
        _lenS2 = 1444 - jax.random.randint(jax.random.fold_in(_rk, 8), (32,), 0, max(1, 1444 // 4) + 1, jnp.int32)
        _ctx_1024P = jax.random.normal(jax.random.fold_in(_rk, 11), (32, 16, 128), jnp.float32)
        _ctx_1024c = jax.random.dirichlet(jax.random.fold_in(_rk, 511), 0.3 * jnp.ones((16,), jnp.float32), (32, 1444))
        _ctx_1024t = jnp.einsum('bsk,bkd->bsd', _ctx_1024c, _ctx_1024P)
        _ctx_1024t = _ctx_1024t * jax.lax.rsqrt(jnp.mean(jnp.square(_ctx_1024t)) + 1e-12) * 0.953939
        ctx_1024 = 2.81802e-05 + 1.00001 * (_ctx_1024t + 0.3 * jax.random.normal(jax.random.fold_in(_rk, 611), (32, 1444, 128), jnp.float32))
        _validS = jnp.arange(100)[None, :] < _lenS[:, None]
        _validS2 = jnp.arange(1444)[None, :] < _lenS2[:, None]
        _causal = jnp.tril(jnp.ones((100, 100), dtype=bool))
        mask_BxS2_bf1 = jnp.ones((32, 1444), dtype=bool)
        _g = jax.random.normal(jax.random.fold_in(_rk, 9001), (2, 2), jnp.float32)
        _g = jnp.sign(_g) * jnp.maximum(jnp.abs(_g), 1.0) + (_g == 0) * 1.0
        g_xattn = _g[0]
        g_ffn = _g[1]
        return (x, ctx_1024, mask_BxS2_bf1, g_xattn, g_ffn)
    x, ctx_1024, mask_BxS2_bf1, g_xattn, g_ffn = _rec_inputs()

    def _L0_xattn_setup():
        import jax, jax.numpy as jnp
        import numpy as np
        E = 128
        NUM_HEADS = 16
        DK = E // NUM_HEADS
        EPS = 1e-05
        NEG_INF = -jnp.inf

        def layer_norm(x, g, b):
            mu = jnp.mean(x, axis=-1, keepdims=True)
            var = jnp.var(x, axis=-1, keepdims=True)
            return (x - mu) * jax.lax.rsqrt(var + EPS) * g + b

        def self_attn(x, Wq, Wk, Wv):
            Q, K, V = (x @ Wq, x @ Wk, x @ Wv)
            energy = jnp.einsum('bqd,bkd->bqk', Q, K)
            S = energy.shape[-1]
            lengths = jnp.sum(energy[:, 0] != 0, axis=-1)
            kidx = jnp.arange(S)
            pad = kidx[None, None, :] >= lengths[:, None, None]
            causal = kidx[None, :] < kidx[:, None]
            causal = (kidx[None, :] > kidx[:, None])[None]
            energy = jnp.where(pad | causal, NEG_INF, energy)
            score = jax.nn.softmax(energy / np.sqrt(DK), axis=-1)
            return jnp.einsum('bqk,bkd->bqd', score, V)

        def cross_attn(x, context, Wq, Wk, Wv):
            Q = x @ Wq
            K, V = (context @ Wk, context @ Wv)
            energy = jnp.einsum('bqd,bkd->bqk', Q, K)
            Sk = energy.shape[-1]
            lengths = jnp.sum(energy[:, 0] != 0, axis=-1)
            kidx = jnp.arange(Sk)
            pad = kidx[None, None, :] >= lengths[:, None, None]
            energy = jnp.where(pad, NEG_INF, energy)
            score = jax.nn.softmax(energy / np.sqrt(DK), axis=-1)
            return jnp.einsum('bqk,bkd->bqd', score, V)
        key = jax.random.key(seed)
        ks = jax.random.split(key, 12)
        B, S = (8, 256)
        s = 1.0 / np.sqrt(E)
        inp = {'x': jax.random.normal(ks[0], (B, S, E), jnp.float32), 'context': jax.random.normal(ks[1], (B, S, E), jnp.float32), 'Wq1': jax.random.normal(ks[2], (E, E), jnp.float32) * s, 'Wk1': jax.random.normal(ks[3], (E, E), jnp.float32) * s, 'Wv1': jax.random.normal(ks[4], (E, E), jnp.float32) * s, 'Wq2': jax.random.normal(ks[5], (E, E), jnp.float32) * s, 'Wk2': jax.random.normal(ks[6], (E, E), jnp.float32) * s, 'Wv2': jax.random.normal(ks[7], (E, E), jnp.float32) * s, 'fc1_w': jax.random.normal(ks[8], (E, E), jnp.float32) * s, 'fc1_b': jnp.zeros((E,), jnp.float32), 'fc2_w': jax.random.normal(ks[9], (E, E), jnp.float32) * s, 'fc2_b': jnp.zeros((E,), jnp.float32), 'ln1_g': jnp.ones((E,), jnp.float32), 'ln1_b': jnp.zeros((E,), jnp.float32), 'ln2_g': jnp.ones((E,), jnp.float32), 'ln2_b': jnp.zeros((E,), jnp.float32), 'ln3_g': jnp.ones((E,), jnp.float32), 'ln3_b': jnp.zeros((E,), jnp.float32)}
        return inp
    _L0_xattn_all = _L0_xattn_setup()
    _L0_xattn_in = {k: v for k, v in _L0_xattn_all.items() if k in ('Wq1', 'Wk1', 'Wv1', 'Wq2', 'Wk2', 'Wv2', 'fc1_w', 'fc1_b', 'fc2_w', 'fc2_b', 'ln1_g', 'ln1_b', 'ln2_g', 'ln2_b', 'ln3_g', 'ln3_b')}
    del _L0_xattn_all

    def _L0_ffn_setup():
        import jax, jax.numpy as jnp
        import numpy as np
        HIDDEN = 128
        INNER = 512

        def _weight_quant(w):
            scale = 1.0 / jnp.clip(jnp.mean(jnp.abs(w)), 1e-05)
            wq = jnp.clip(jnp.round(w * scale), -1.0, 1.0) / scale
            return w + jax.lax.stop_gradient(wq - w)

        def _act_quant(x):
            scale = 127.0 / jnp.clip(jnp.max(jnp.abs(x), axis=-1, keepdims=True), 1e-05)
            xq = jnp.clip(jnp.round(x * scale), -128.0, 127.0) / scale
            return x + jax.lax.stop_gradient(xq - x)

        def _bitlinear(x, w):
            return jnp.einsum('bsi,oi->bso', _act_quant(x), _weight_quant(w))
        key = jax.random.key(seed)
        k0, k1, k2, k3 = jax.random.split(key, 4)
        x = jax.random.normal(k0, (4, 256, HIDDEN), dtype=jnp.float32)
        w_gate = jax.random.normal(k1, (INNER, HIDDEN), dtype=jnp.float32) / np.sqrt(HIDDEN)
        w_up = jax.random.normal(k2, (INNER, HIDDEN), dtype=jnp.float32) / np.sqrt(HIDDEN)
        w_down = jax.random.normal(k3, (HIDDEN, INNER), dtype=jnp.float32) / np.sqrt(INNER)
        return {'x': x, 'w_gate': w_gate, 'w_up': w_up, 'w_down': w_down}
    _L0_ffn_all = _L0_ffn_setup()
    _L0_ffn_in = {k: v for k, v in _L0_ffn_all.items() if k in ('w_gate', 'w_up', 'w_down')}
    del _L0_ffn_all

    def _L1_xattn_setup():
        import jax, jax.numpy as jnp
        import numpy as np
        N_HEADS = 16
        D_MODEL = 128
        HEAD_DIM = D_MODEL // N_HEADS
        MASK_FILL = -100000000.0

        def _split_heads(x):
            B, S, _ = x.shape
            return x.reshape(B, S, N_HEADS, HEAD_DIM).transpose(0, 2, 1, 3)
        key = jax.random.key(seed)
        ks = jax.random.split(key, 12)
        B, L, P = (2, 256, 256)
        s = 1.0 / np.sqrt(D_MODEL).astype(np.float32)
        inp = {'q': jax.random.normal(ks[0], (B, L, D_MODEL), dtype=jnp.float32), 'k': jax.random.normal(ks[1], (B, P, D_MODEL), dtype=jnp.float32), 'v': jax.random.normal(ks[2], (B, P, D_MODEL), dtype=jnp.float32), 'attention_mask': jnp.ones((B, P), dtype=bool), 'Wq': jax.random.normal(ks[3], (D_MODEL, D_MODEL), dtype=jnp.float32) * s, 'bq': jnp.zeros((D_MODEL,), dtype=jnp.float32), 'Wk': jax.random.normal(ks[4], (D_MODEL, D_MODEL), dtype=jnp.float32) * s, 'bk': jnp.zeros((D_MODEL,), dtype=jnp.float32), 'Wv': jax.random.normal(ks[5], (D_MODEL, D_MODEL), dtype=jnp.float32) * s, 'bv': jnp.zeros((D_MODEL,), dtype=jnp.float32), 'Wo': jax.random.normal(ks[6], (D_MODEL, D_MODEL), dtype=jnp.float32) * s, 'bo': jnp.zeros((D_MODEL,), dtype=jnp.float32)}
        return inp
    _L1_xattn_all = _L1_xattn_setup()
    _L1_xattn_in = {k: v for k, v in _L1_xattn_all.items() if k in ('Wq', 'bq', 'Wk', 'bk', 'Wv', 'bv', 'Wo', 'bo')}
    del _L1_xattn_all

    def _L1_ffn_setup():
        import jax, jax.numpy as jnp
        import numpy as np
        D_MODEL = 128
        NHEAD = 16
        HEAD_DIM = D_MODEL // NHEAD
        FF = 256
        NUM_EXPERTS = 8
        EPS = 1e-05

        def _ln(x, g, b):
            m = x.mean(-1, keepdims=True)
            v = ((x - m) ** 2).mean(-1, keepdims=True)
            return (x - m) / jnp.sqrt(v + EPS) * g + b

        def _attention(src, Wq, bq, Wk, bk, Wv, bv, Wo, bo):
            B, T, d = src.shape
            scale = HEAD_DIM ** (-0.5)
            q = (src @ Wq + bq).reshape(B, T, NHEAD, HEAD_DIM)
            k = (src @ Wk + bk).reshape(B, T, NHEAD, HEAD_DIM)
            v = (src @ Wv + bv).reshape(B, T, NHEAD, HEAD_DIM)
            scores = jnp.einsum('bqhd,bkhd->bhqk', q, k) * scale
            probs = jax.nn.softmax(scores, axis=-1)
            out = jnp.einsum('bhqk,bkhd->bqhd', probs, v).reshape(B, T, d)
            return out @ Wo + bo

        def _moe(x, gW, gb, W1, b1, W2, b2):
            B, T, d = x.shape
            xf = x.reshape(-1, d)
            gates = jax.nn.softmax(xf @ gW + gb, axis=-1)
            top2_scores, top2_idx = jax.lax.top_k(gates, 2)
            w = (jax.nn.one_hot(top2_idx, NUM_EXPERTS, dtype=xf.dtype) * top2_scores[..., None]).sum(1)
            h = jax.nn.relu(jnp.einsum('nd,edf->enf', xf, W1) + b1[:, None, :])
            y = jnp.einsum('enf,efd->end', h, W2) + b2[:, None, :]
            out = jnp.einsum('ne,end->nd', w, y)
            return out.reshape(B, T, d)
        key = jax.random.key(seed)
        ks = jax.random.split(key, 12)
        s = 0.02
        d, f, E = (D_MODEL, FF, NUM_EXPERTS)
        return {'src': jax.random.normal(ks[0], (8, 64, d), dtype=jnp.float32), 'Wq': jax.random.normal(ks[1], (d, d), dtype=jnp.float32) * s, 'bq': jnp.zeros((d,), jnp.float32), 'Wk': jax.random.normal(ks[2], (d, d), dtype=jnp.float32) * s, 'bk': jnp.zeros((d,), jnp.float32), 'Wv': jax.random.normal(ks[3], (d, d), dtype=jnp.float32) * s, 'bv': jnp.zeros((d,), jnp.float32), 'Wo': jax.random.normal(ks[4], (d, d), dtype=jnp.float32) * s, 'bo': jnp.zeros((d,), jnp.float32), 'gW': jax.random.normal(ks[5], (d, E), dtype=jnp.float32) * s, 'gb': jnp.zeros((E,), jnp.float32), 'W1': jax.random.normal(ks[6], (E, d, f), dtype=jnp.float32) * s, 'b1': jnp.zeros((E, f), jnp.float32), 'W2': jax.random.normal(ks[7], (E, f, d), dtype=jnp.float32) * s, 'b2': jnp.zeros((E, d), jnp.float32), 'ln1_g': jnp.ones((d,), jnp.float32), 'ln1_b': jnp.zeros((d,), jnp.float32), 'ln2_g': jnp.ones((d,), jnp.float32), 'ln2_b': jnp.zeros((d,), jnp.float32)}
    _L1_ffn_all = _L1_ffn_setup()
    _L1_ffn_in = {k: v for k, v in _L1_ffn_all.items() if k in ('Wq', 'bq', 'Wk', 'bk', 'Wv', 'bv', 'Wo', 'bo', 'gW', 'gb', 'W1', 'b1', 'W2', 'b2', 'ln1_g', 'ln1_b', 'ln2_g', 'ln2_b')}
    del _L1_ffn_all
    return {'x': x, 'ctx_1024': ctx_1024, 'mask_BxS2_bf1': mask_BxS2_bf1, 'g_xattn': g_xattn, 'g_ffn': g_ffn, 'L0_xattn_Wq1': _L0_xattn_in['Wq1'], 'L0_xattn_Wk1': _L0_xattn_in['Wk1'], 'L0_xattn_Wv1': _L0_xattn_in['Wv1'], 'L0_xattn_Wq2': _L0_xattn_in['Wq2'], 'L0_xattn_Wk2': _L0_xattn_in['Wk2'], 'L0_xattn_Wv2': _L0_xattn_in['Wv2'], 'L0_xattn_fc1_w': _L0_xattn_in['fc1_w'], 'L0_xattn_fc1_b': _L0_xattn_in['fc1_b'], 'L0_xattn_fc2_w': _L0_xattn_in['fc2_w'], 'L0_xattn_fc2_b': _L0_xattn_in['fc2_b'], 'L0_xattn_ln1_g': _L0_xattn_in['ln1_g'], 'L0_xattn_ln1_b': _L0_xattn_in['ln1_b'], 'L0_xattn_ln2_g': _L0_xattn_in['ln2_g'], 'L0_xattn_ln2_b': _L0_xattn_in['ln2_b'], 'L0_xattn_ln3_g': _L0_xattn_in['ln3_g'], 'L0_xattn_ln3_b': _L0_xattn_in['ln3_b'], 'L0_ffn_w_gate': _L0_ffn_in['w_gate'], 'L0_ffn_w_up': _L0_ffn_in['w_up'], 'L0_ffn_w_down': _L0_ffn_in['w_down'], 'L1_xattn_Wq': _L1_xattn_in['Wq'], 'L1_xattn_bq': _L1_xattn_in['bq'], 'L1_xattn_Wk': _L1_xattn_in['Wk'], 'L1_xattn_bk': _L1_xattn_in['bk'], 'L1_xattn_Wv': _L1_xattn_in['Wv'], 'L1_xattn_bv': _L1_xattn_in['bv'], 'L1_xattn_Wo': _L1_xattn_in['Wo'], 'L1_xattn_bo': _L1_xattn_in['bo'], 'L1_ffn_Wq': _L1_ffn_in['Wq'], 'L1_ffn_bq': _L1_ffn_in['bq'], 'L1_ffn_Wk': _L1_ffn_in['Wk'], 'L1_ffn_bk': _L1_ffn_in['bk'], 'L1_ffn_Wv': _L1_ffn_in['Wv'], 'L1_ffn_bv': _L1_ffn_in['bv'], 'L1_ffn_Wo': _L1_ffn_in['Wo'], 'L1_ffn_bo': _L1_ffn_in['bo'], 'L1_ffn_gW': _L1_ffn_in['gW'], 'L1_ffn_gb': _L1_ffn_in['gb'], 'L1_ffn_W1': _L1_ffn_in['W1'], 'L1_ffn_b1': _L1_ffn_in['b1'], 'L1_ffn_W2': _L1_ffn_in['W2'], 'L1_ffn_b2': _L1_ffn_in['b2'], 'L1_ffn_ln1_g': _L1_ffn_in['ln1_g'], 'L1_ffn_ln1_b': _L1_ffn_in['ln1_b'], 'L1_ffn_ln2_g': _L1_ffn_in['ln2_g'], 'L1_ffn_ln2_b': _L1_ffn_in['ln2_b']}

def reference(x, ctx_1024, mask_BxS2_bf1, g_xattn, g_ffn, L0_xattn_Wq1, L0_xattn_Wk1, L0_xattn_Wv1, L0_xattn_Wq2, L0_xattn_Wk2, L0_xattn_Wv2, L0_xattn_fc1_w, L0_xattn_fc1_b, L0_xattn_fc2_w, L0_xattn_fc2_b, L0_xattn_ln1_g, L0_xattn_ln1_b, L0_xattn_ln2_g, L0_xattn_ln2_b, L0_xattn_ln3_g, L0_xattn_ln3_b, L0_ffn_w_gate, L0_ffn_w_up, L0_ffn_w_down, L1_xattn_Wq, L1_xattn_bq, L1_xattn_Wk, L1_xattn_bk, L1_xattn_Wv, L1_xattn_bv, L1_xattn_Wo, L1_xattn_bo, L1_ffn_Wq, L1_ffn_bq, L1_ffn_Wk, L1_ffn_bk, L1_ffn_Wv, L1_ffn_bv, L1_ffn_Wo, L1_ffn_bo, L1_ffn_gW, L1_ffn_gb, L1_ffn_W1, L1_ffn_b1, L1_ffn_W2, L1_ffn_b2, L1_ffn_ln1_g, L1_ffn_ln1_b, L1_ffn_ln2_g, L1_ffn_ln2_b):
    import jax
    import jax.numpy as jnp

    def _L0_xattn_ref(x, context, Wq1, Wk1, Wv1, Wq2, Wk2, Wv2, fc1_w, fc1_b, fc2_w, fc2_b, ln1_g, ln1_b, ln2_g, ln2_b, ln3_g, ln3_b):
        import jax, jax.numpy as jnp
        import numpy as np
        E = 128
        NUM_HEADS = 16
        DK = E // NUM_HEADS
        EPS = 1e-05
        NEG_INF = -jnp.inf

        def layer_norm(x, g, b):
            mu = jnp.mean(x, axis=-1, keepdims=True)
            var = jnp.var(x, axis=-1, keepdims=True)
            return (x - mu) * jax.lax.rsqrt(var + EPS) * g + b

        def self_attn(x, Wq, Wk, Wv):
            Q, K, V = (x @ Wq, x @ Wk, x @ Wv)
            energy = jnp.einsum('bqd,bkd->bqk', Q, K)
            S = energy.shape[-1]
            lengths = jnp.sum(energy[:, 0] != 0, axis=-1)
            kidx = jnp.arange(S)
            pad = kidx[None, None, :] >= lengths[:, None, None]
            causal = kidx[None, :] < kidx[:, None]
            causal = (kidx[None, :] > kidx[:, None])[None]
            energy = jnp.where(pad | causal, NEG_INF, energy)
            score = jax.nn.softmax(energy / np.sqrt(DK), axis=-1)
            return jnp.einsum('bqk,bkd->bqd', score, V)

        def cross_attn(x, context, Wq, Wk, Wv):
            Q = x @ Wq
            K, V = (context @ Wk, context @ Wv)
            energy = jnp.einsum('bqd,bkd->bqk', Q, K)
            Sk = energy.shape[-1]
            lengths = jnp.sum(energy[:, 0] != 0, axis=-1)
            kidx = jnp.arange(Sk)
            pad = kidx[None, None, :] >= lengths[:, None, None]
            energy = jnp.where(pad, NEG_INF, energy)
            score = jax.nn.softmax(energy / np.sqrt(DK), axis=-1)
            return jnp.einsum('bqk,bkd->bqd', score, V)
        z = self_attn(x, Wq1, Wk1, Wv1)
        x = layer_norm(x + z, ln1_g, ln1_b)
        z = cross_attn(x, context, Wq2, Wk2, Wv2)
        x = layer_norm(x + z, ln2_g, ln2_b)
        z = jax.nn.relu(x @ fc1_w + fc1_b)
        z = z @ fc2_w + fc2_b
        return layer_norm(x + z, ln3_g, ln3_b)

    def _L0_ffn_ref(x, w_gate, w_up, w_down):
        import jax, jax.numpy as jnp
        import numpy as np
        HIDDEN = 128
        INNER = 512

        def _weight_quant(w):
            scale = 1.0 / jnp.clip(jnp.mean(jnp.abs(w)), 1e-05)
            wq = jnp.clip(jnp.round(w * scale), -1.0, 1.0) / scale
            return w + jax.lax.stop_gradient(wq - w)

        def _act_quant(x):
            scale = 127.0 / jnp.clip(jnp.max(jnp.abs(x), axis=-1, keepdims=True), 1e-05)
            xq = jnp.clip(jnp.round(x * scale), -128.0, 127.0) / scale
            return x + jax.lax.stop_gradient(xq - x)

        def _bitlinear(x, w):
            return jnp.einsum('bsi,oi->bso', _act_quant(x), _weight_quant(w))
        gate = jax.nn.silu(_bitlinear(x, w_gate))
        up = _bitlinear(x, w_up)
        return _bitlinear(gate * up, w_down)

    def _L1_xattn_ref(q, k, v, attention_mask, Wq, bq, Wk, bk, Wv, bv, Wo, bo):
        import jax, jax.numpy as jnp
        import numpy as np
        N_HEADS = 16
        D_MODEL = 128
        HEAD_DIM = D_MODEL // N_HEADS
        MASK_FILL = -100000000.0

        def _split_heads(x):
            B, S, _ = x.shape
            return x.reshape(B, S, N_HEADS, HEAD_DIM).transpose(0, 2, 1, 3)
        qm = _split_heads(q @ Wq.T + bq)
        km = _split_heads(k @ Wk.T + bk)
        vm = _split_heads(v @ Wv.T + bv)
        scores = jnp.einsum('bnlh,bnph->bnlp', qm, km) / np.sqrt(HEAD_DIM).astype(np.float32)
        mask = attention_mask[:, None, None, :]
        scores = jnp.where(mask, scores, MASK_FILL)
        attn = jax.nn.softmax(scores, axis=-1)
        out = jnp.einsum('bnlp,bnph->bnlh', attn, vm)
        B, _, L, _ = out.shape
        out = out.transpose(0, 2, 1, 3).reshape(B, L, D_MODEL)
        return out @ Wo.T + bo

    def _L1_ffn_ref(src, Wq, bq, Wk, bk, Wv, bv, Wo, bo, gW, gb, W1, b1, W2, b2, ln1_g, ln1_b, ln2_g, ln2_b):
        import jax, jax.numpy as jnp
        import numpy as np
        D_MODEL = 128
        NHEAD = 16
        HEAD_DIM = D_MODEL // NHEAD
        FF = 256
        NUM_EXPERTS = 8
        EPS = 1e-05

        def _ln(x, g, b):
            m = x.mean(-1, keepdims=True)
            v = ((x - m) ** 2).mean(-1, keepdims=True)
            return (x - m) / jnp.sqrt(v + EPS) * g + b

        def _attention(src, Wq, bq, Wk, bk, Wv, bv, Wo, bo):
            B, T, d = src.shape
            scale = HEAD_DIM ** (-0.5)
            q = (src @ Wq + bq).reshape(B, T, NHEAD, HEAD_DIM)
            k = (src @ Wk + bk).reshape(B, T, NHEAD, HEAD_DIM)
            v = (src @ Wv + bv).reshape(B, T, NHEAD, HEAD_DIM)
            scores = jnp.einsum('bqhd,bkhd->bhqk', q, k) * scale
            probs = jax.nn.softmax(scores, axis=-1)
            out = jnp.einsum('bhqk,bkhd->bqhd', probs, v).reshape(B, T, d)
            return out @ Wo + bo

        def _moe(x, gW, gb, W1, b1, W2, b2):
            B, T, d = x.shape
            xf = x.reshape(-1, d)
            gates = jax.nn.softmax(xf @ gW + gb, axis=-1)
            top2_scores, top2_idx = jax.lax.top_k(gates, 2)
            w = (jax.nn.one_hot(top2_idx, NUM_EXPERTS, dtype=xf.dtype) * top2_scores[..., None]).sum(1)
            h = jax.nn.relu(jnp.einsum('nd,edf->enf', xf, W1) + b1[:, None, :])
            y = jnp.einsum('enf,efd->end', h, W2) + b2[:, None, :]
            out = jnp.einsum('ne,end->nd', w, y)
            return out.reshape(B, T, d)
        attn_out = _attention(src, Wq, bq, Wk, bk, Wv, bv, Wo, bo)
        x = _ln(src + attn_out, ln1_g, ln1_b)
        ff = _moe(x, gW, gb, W1, b1, W2, b2)
        return _ln(x + ff, ln2_g, ln2_b)
    x = x + jnp.tanh(g_xattn[0]) * _L0_xattn_ref(_layernorm(x, axis=-1), ctx_1024, L0_xattn_Wq1, L0_xattn_Wk1, L0_xattn_Wv1, L0_xattn_Wq2, L0_xattn_Wk2, L0_xattn_Wv2, L0_xattn_fc1_w, L0_xattn_fc1_b, L0_xattn_fc2_w, L0_xattn_fc2_b, L0_xattn_ln1_g, L0_xattn_ln1_b, L0_xattn_ln2_g, L0_xattn_ln2_b, L0_xattn_ln3_g, L0_xattn_ln3_b)
    x = x + jnp.tanh(g_ffn[0]) * _L0_ffn_ref(_layernorm(x, axis=-1), L0_ffn_w_gate, L0_ffn_w_up, L0_ffn_w_down)
    x = x + jnp.tanh(g_xattn[1]) * _L1_xattn_ref(_layernorm(x, axis=-1), ctx_1024, ctx_1024, mask_BxS2_bf1, L1_xattn_Wq, L1_xattn_bq, L1_xattn_Wk, L1_xattn_bk, L1_xattn_Wv, L1_xattn_bv, L1_xattn_Wo, L1_xattn_bo)
    x = x + jnp.tanh(g_ffn[1]) * _L1_ffn_ref(_layernorm(x, axis=-1), L1_ffn_Wq, L1_ffn_bq, L1_ffn_Wk, L1_ffn_bk, L1_ffn_Wv, L1_ffn_bv, L1_ffn_Wo, L1_ffn_bo, L1_ffn_gW, L1_ffn_gb, L1_ffn_W1, L1_ffn_b1, L1_ffn_W2, L1_ffn_b2, L1_ffn_ln1_g, L1_ffn_ln1_b, L1_ffn_ln2_g, L1_ffn_ln2_b)
    return x

_drawn_inputs = setup_inputs


def setup_inputs(seed=0):
    import zlib

    import numpy as np

    out = dict(_drawn_inputs(seed))
    spreads = {'g_ffn': (-1.0, 0.2),
     'L0_xattn_fc1_b': (0.0, 0.331),
     'L0_xattn_fc2_b': (0.0, 0.1),
     'L0_xattn_ln1_g': (1.0, 0.2),
     'L0_xattn_ln1_b': (0.0, 0.1),
     'L0_xattn_ln2_g': (1.0, 0.2),
     'L0_xattn_ln2_b': (0.0, 0.1),
     'L0_xattn_ln3_g': (1.0, 0.2),
     'L0_xattn_ln3_b': (0.0, 0.1),
     'L1_xattn_bq': (0.0, 0.624),
     'L1_xattn_bk': (0.0, 0.8),
     'L1_xattn_bv': (0.0, 0.1),
     'L1_xattn_bo': (0.0, 0.1),
     'L1_ffn_bq': (0.0, 0.8),
     'L1_ffn_bk': (0.0, 0.8),
     'L1_ffn_bv': (0.0, 0.384),
     'L1_ffn_bo': (0.0, 0.1),
     'L1_ffn_gb': (0.0, 0.51),
     'L1_ffn_b1': (0.0, 0.8),
     'L1_ffn_b2': (0.0, 0.357),
     'L1_ffn_ln1_g': (1.0, 0.2),
     'L1_ffn_ln1_b': (0.0, 0.1),
     'L1_ffn_ln2_g': (1.0, 0.2),
     'L1_ffn_ln2_b': (0.0, 0.1)}
    factors = {'L1_ffn_Wq': 8.0,
     'L1_ffn_Wk': 8.0,
     'L1_ffn_Wv': 2.896,
     'L1_ffn_W1': 6.015,
     'L1_ffn_W2': 4.548}
    for name, (base, spread) in spreads.items():
        noise = np.random.default_rng([zlib.crc32(name.encode()), seed]).standard_normal(out[name].shape)
        drawn = base * np.exp(spread * noise) if base else spread * noise
        out[name] = jnp.asarray(drawn.astype(out[name].dtype))
    for name, factor in factors.items():
        out[name] = (out[name] * factor).astype(out[name].dtype)
    return out
```

```python
from contextlib import ExitStack

import concourse.bass as bass
from concourse import mybir

F32 = mybir.dt.float32
F32R = mybir.dt.float32r
BF16 = mybir.dt.bfloat16
U8 = mybir.dt.uint8
U32 = mybir.dt.uint32
ALU = mybir.AluOpType
ACT = mybir.ActivationFunctionType
AX = mybir.AxisListType

D = 128
T = 100
S = 1444
BATCH = 32
GROUP = 4
GROUPS = BATCH // GROUP
TG = GROUP * T
HEADS, HD = 16, 8
HG = 4
HQ = HEADS * T
KT = -(-S // D)
REST = S - (KT - 1) * D
CHUNK = 482
SPAD = 3 * CHUNK
PADK = KT * D
CHUNKS = [(c * CHUNK, min(CHUNK, S - c * CHUNK)) for c in range(3)]
QCH = -(-HQ // D)
INNER = 512
EXPERTS, FF = 8, 256
FT = EXPERTS * FF // D
EPS = 1e-5
DK_SCALE = float(HD) ** -0.5
ROUND = 12582912.0
PENALTY = float(2 ** 27)
CUT = 1e30
STACK = 99
JOBS = 3 + 3 + 3 * QCH + 1
LNS = 9
TURNS = 8
KS_DMAS = 13
DVE_LINKS = 151

WNAMES = ["q1T", "k1T", "q2T", "k2T", "v1", "v2", "fc1", "fc2", "xqT", "xkT", "xvT", "xoT", "fq", "fk", "fv", "fo"]
WCOL = {n: i * D for i, n in enumerate(WNAMES)}
WSTACK = len(WNAMES) * D
WGATE = WSTACK + 4 * 96
WPACK = WGATE + EXPERTS
CNAMES = ["fc1", "xq", "xk", "xv", "fq", "fk", "fv"]
CCOL = {n: i for i, n in enumerate(CNAMES)}
CB1 = len(CNAMES)
CSTACK = CB1 + FT
CPACK = CSTACK + 4
RNAMES = ["ln1g", "ln1b", "ln2g", "ln2b", "ln3g", "ln3b", "fc2b", "xbo", "fbo", "fln1g", "fln1b", "fln2g", "fln2b"]
RROW = {n: i * D for i, n in enumerate(RNAMES)}
RGB = len(RNAMES) * D
RTANH = RGB + EXPERTS
RPACK = RTANH + 4
K_ID, K_M16, K_M4, K_NEG1, K_BASE, K_IOTA, K_LAST = 0, 128, 144, 148, 149, 249, 257
KPACK = K_LAST + 32

SIGNALS = """
consts_loaded big_loaded pen_stored cleared x_loaded out_stored
m_turn_psum m_ready wsum_psum wsum_ready wq_ready tanh_ready pen_ready0 ones_ready
var_ready rstd_ready tok_ready tok_turned tokT_ready
r_psum rT_ready v1_psum v1_ready s1_psum len1_ready len1_psum sm1_ready e1_ready e1T_psum e1T_ready z1_psum
s2_psum row_ready s2m_psum max2_ready e2_ready pT_psum pT_ready z2T_psum z2T_ready z2_psum
f1_psum f1_ready f2_psum factors_ready gu_psum eg_ready gu_used aq_ready aqT_psum aqT_ready down_psum
q_psum q_ready qs_psum qs_ready qbd_ready qexp_ready ring_filled ring_drained kl_ready kh_ready mx_ready nm_ready
st_psum pt_ready pv_done att_free att_ready attx_psum
fqk_psum fq_ready fk_ready fv_psum fv_ready kbd_ready fs_psum fs_used fsub_ready fe_ready feT_psum feT_ready fo_psum fo_used
wo_psum gate_psum gsub_ready gexp_ready w_ready wT_psum wT_ready b2_psum moe_h_psum moe_h_ready moe_y_psum moe_y_used out_ready
""".split()


def build(nc, x, ctxn, ctxt, mask, wpack, cpack, rpack, kpack, w1, w2, b2, wgu, out):
    ctx = ExitStack()
    with ctx:
        def sb(name, shape, dt=F32):
            return ctx.enter_context(nc.sbuf_tensor(name, shape, dt))

        sem = {n: ctx.enter_context(nc.semaphore(n)) for n in SIGNALS}
        ct_loaded = [ctx.enter_context(nc.semaphore(f"ct_loaded{p}")) for p in range(2)]
        cn_loaded = [ctx.enter_context(nc.semaphore(f"cn_loaded{p}")) for p in range(2)]
        ks_loaded = [ctx.enter_context(nc.semaphore(f"ks_loaded{p}")) for p in range(2)]
        qrow_loaded = [ctx.enter_context(nc.semaphore(f"qrow_loaded{p}")) for p in range(2)]
        mask_loaded = [ctx.enter_context(nc.semaphore(f"mask_loaded{p}")) for p in range(2)]
        dve_chain = ctx.enter_context(nc.semaphore("dve_chain"))
        psum = ctx.enter_context(nc.psum_tensor("psum", [D, 8, 512], F32))
        pen_dram = nc.dram_tensor("pen_scratch", [BATCH, S], F32, kind="Internal").ap()

        W = sb("W", [D, WPACK])
        C = sb("C", [D, CPACK])
        R = sb("R", [T, RPACK])
        K = sb("K", [D, KPACK])
        W1 = sb("W1", [D, FT * D])
        W2 = sb("W2", [D, FT * D])
        B2 = sb("B2", [EXPERTS, D])
        M12 = sb("M12", [D, 2 * D])
        wq_int = sb("wq_int", [D, 3 * INNER], BF16)
        wscale = sb("wscale", [D, 12])
        tanhs = sb("tanhs", [T, 4])
        ones = sb("ones", [D, D])
        ones_row = sb("ones_row", [1, D], BF16)
        cut_row = sb("cut_row", [1, D], BF16)
        key_row = sb("key_row", [1, SPAD])
        half = sb("half", [T, GROUP])
        xbq = sb("xbq", [D, 8])
        X = sb("X", [T, GROUP, D])
        H = sb("H", [T, GROUP, D])
        U = sb("U", [T, GROUP, D])
        Y = sb("Y", [T, GROUP, D])
        VS = sb("VS", [T, GROUP, D])
        HT = sb("HT", [D, TG])
        RT = sb("RT", [D, TG])
        HQT = sb("HQT", [D, TG], BF16)
        AT = sb("AT", [D, TG])
        E1 = sb("E1", [T, GROUP, T])
        E1T = sb("E1T", [T, TG])
        st = sb("st", [T, GROUP, 6])
        mv = sb("mv", [T, GROUP, 2])
        ve = sb("ve", [T, GROUP])
        rs = sb("rs", [T, GROUP])
        sm = sb("sm", [T, 16, GROUP])
        len1 = sb("len1", [1, GROUP])
        len2 = sb("len2", [1, 1])
        prow = sb("prow", [1, SPAD], BF16)
        CT = sb("CT", [D, 2, SPAD])
        CN = sb("CN", [D, 2, KT, D])
        MB = sb("MB", [D, 2, S], U8)
        KT32 = sb("KT32", [D, SPAD])
        KH = sb("KH", [D, S], F32R)
        KL = sb("KL", [D, HQ], F32R)
        KS = sb("KS", [D, 2, HG, PADK], F32R)
        QBD = sb("QBD", [D, QCH * D], F32R)
        QS = sb("QS", [D, 2, QCH * D], F32R)
        QR = sb("QR", [96, HG, TG])
        T32 = sb("T32", [D, HG, TG])
        PT = sb("PT", [D, 2, HG, TG])
        mx = sb("mx", [D, 16])
        NMH = sb("NMH", [QCH, D], F32R)
        NML = sb("NML", [QCH, D], F32R)
        carrier = sb("carrier", [1, 1])
        sm4 = sb("sm4", [D, HG, T])
        dn = sb("dn", [T, 4, HEADS])
        gt = sb("gt", [T, 6, GROUP * EXPERTS])
        gi = sb("gi", [T, GROUP * EXPERTS], U32)

        PJ = KT32
        V = CN
        WT = E1T[0:EXPERTS, :]
        HE = T32[:, 0:2, :]
        EGT = T32[0:T, :, :].rearrange("p a b -> p (a b)")[:, 0:INNER]
        AQ = T32[0:T, :, :].rearrange("p a b -> p (a b)")[:, INNER:2 * INNER]
        PTA = T32[:, :, :].rearrange("p a b -> p (a b)")[:, 0:KT * T].rearrange("p (k t) -> p k t", k=KT)
        AQT = sb("AQT", [D, TG], BF16)
        KBD = T32[:, :, :].rearrange("p a b -> p (a b)")
        SM2 = PT[0:T, 0, :, :].rearrange("p a b -> p (a b)")
        PT2 = PT[0:T, 1, :, :].rearrange("p a b -> p (a b)")
        WRAW = PT[:, 0, :, :].rearrange("p a b -> p (a b)")[:, 0:3 * INNER]
        WTMP = PT[:, 1, :, :].rearrange("p a b -> p (a b)")[:, 0:3 * INNER]
        PEN = T32[0:BATCH, :, :].rearrange("p a b -> p (a b)")[:, 0:S]
        PENR = KL[0:BATCH, 0:S]

        ident = K[:, K_ID:K_ID + D]
        mask16 = K[:, K_M16:K_M16 + HEADS]
        mask4 = K[:, K_M4:K_M4 + HG]

        def w(name):
            return W[:, WCOL[name]:WCOL[name] + D]

        def col(name):
            return C[:, CCOL[name]:CCOL[name] + 1]

        def row(name):
            return R[:, RROW[name]:RROW[name] + D].unsqueeze(1).to_broadcast([T, GROUP, D])

        def bank(b, rows=D, cols=512, at=0):
            return psum[0:rows, b, at:at + cols]

        def tok_bank(b):
            return psum[0:T, b, :].rearrange("p (j d) -> p j d", j=GROUP)

        def ts_(j, n=T):
            return slice(j * n, (j + 1) * n)

        block = ctx.enter_context(nc.Block())

        @block.sync
        def _(sp):
            for dst, src in ((W, wpack), (C, cpack), (K, kpack), (R, rpack.partition_broadcast(T)),
                             (WRAW, wgu)):
                sp.dma_start(dst[:, :], src).then_inc(sem["consts_loaded"], 16)
            sp.dma_start(MB[0:BATCH, 0, :], mask).then_inc(sem["consts_loaded"], 16)
            sp.dma_start(W1[:, :], w1).then_inc(sem["big_loaded"], 16)
            sp.dma_start(W2[:, :], w2).then_inc(sem["big_loaded"], 16)
            sp.dma_start(B2[:, :], b2).then_inc(sem["big_loaded"], 16)
            sp.wait_ge(sem["pen_ready0"], 1)
            sp.dma_start(pen_dram, PENR.bitcast(F32)).then_inc(sem["pen_stored"], 16)
            sp.wait_ge(sem["pen_stored"], 16)
            with sp.Fori(0, GROUPS) as g:
                sp.wait_ge(sem["out_ready"], g + 1)
                sp.dma_start(X[:, :, :], x[:, bass.ds(g * GROUP, GROUP), :]).then_inc(sem["x_loaded"], 16)

                def load_ct(n):
                    if 2 <= n < 6:
                        sp.wait_ge(sem["s2_psum"], g * GROUP + (n - 1))
                    elif n >= 6:
                        sp.wait_ge(sem["ring_filled"], (g * GROUP + (n - 6)) * JOBS + 6)
                    sp.dma_start(CT[:, n % 2, 0:S], ctxt[g * GROUP + n % GROUP]).then_inc(ct_loaded[n % 2], 16)

                def load_cn(j):
                    if j >= 2:
                        sp.wait_ge(sem["z2T_psum"], g * GROUP + j - 1)
                    src = ctxn[g * GROUP + j]
                    sp.dma_start(CN[:, j % 2, 0:KT - 1, :],
                                 src[0:(KT - 1) * D, :].rearrange("(k p) d -> p k d", p=D)).then_inc(cn_loaded[j % 2], 16)
                    sp.dma_start(CN[0:REST, j % 2, KT - 1, :], src[(KT - 1) * D:S, :]).then_inc(cn_loaded[j % 2], 16)

                for j in range(GROUP):
                    load_ct(j)
                    load_cn(j)
                load_ct(GROUP)
                load_ct(GROUP + 1)

                def load_mask(j):
                    sp.dma_start(MB[:, j % 2, :], mask[g * GROUP + j].partition_broadcast(D)).then_inc(mask_loaded[j % 2], 16)

                load_mask(0)
                load_mask(1)
                for j in range(GROUP):
                    n = g * GROUP + j
                    sp.wait_ge(sem["kl_ready"], g * GROUP + j + 1)
                    for hg in range(HG):
                        for t, part in enumerate((KH, KH, KL)):
                            sp.dma_start(KS[32 * t:32 * t + 32, j % 2, hg, 0:S].bitcast(F32),
                                         part[32 * hg:32 * hg + 32, 0:S].bitcast(F32)).then_inc(ks_loaded[j % 2], 16)
                    sp.dma_start(KS[98:99, j % 2, :, 0:S].bitcast(F32),
                                 pen_dram[bass.ds(n, 1), :].unsqueeze(1).to_broadcast([1, HG, S]))\
                      .then_inc(ks_loaded[j % 2], 16)
                    if j + 2 < GROUP:
                        load_ct(GROUP + j + 2)
                    sp.wait_ge(sem["nm_ready"], g * GROUP + j + 1)
                    for n, part in enumerate((NMH, NML)):
                        sp.dma_start(QS[96 + n:97 + n, j % 2, :].bitcast(F32), part[:, :].bitcast(F32)).then_inc(qrow_loaded[j % 2], 16)
                    if j + 2 < GROUP:
                        load_mask(j + 2)
                sp.wait_ge(sem["out_ready"], g + 2)
                sp.dma_start(out[:, bass.ds(g * GROUP, GROUP), :], Y[:, :, :]).then_inc(sem["out_stored"], 16)
            sp.wait_ge(sem["out_stored"], GROUPS * 16)

        @block.gpsimd
        def _(pool):
            nc.gpsimd.memset(half[:, :], -0.5)
            nc.gpsimd.memset(ones[:, :], 1.0)
            nc.gpsimd.memset(ones_row[:, :], 1.0)
            nc.gpsimd.memset(cut_row[:, :], CUT)
            nc.gpsimd.memset(CT[:, :, S:SPAD], 0.0)
            nc.gpsimd.memset(KS[:, :, :, :].bitcast(F32), 0.0)
            nc.gpsimd.memset(QS[:, :, :].bitcast(F32), 0.0)
            nc.gpsimd.memset(QBD[:, HQ:].bitcast(F32), 0.0)
            nc.gpsimd.memset(mx[:, :], 0.0)
            nc.gpsimd.iota(key_row[:, :], [[-1, SPAD]], base=0, channel_multiplier=0,
                           allow_small_or_imprecise_dtypes=True).then_inc(sem["ones_ready"], 1)
            pool.wait_ge(sem["ones_ready"], 1)
            nc.gpsimd.memset(KS[96:98, :, :, :].bitcast(F32), 1.0)
            nc.gpsimd.memset(QS[96:STACK, :, :].bitcast(F32), 1.0).then_inc(sem["cleared"], 1)
            with pool.Fori(0, GROUPS) as g:
                for k in range(LNS):
                    pool.wait_ge(sem["var_ready"], g * LNS + k + 1)
                    nc.gpsimd.tensor_tensor(rs[:, :], ve[:, :], half[:, :], ALU.pow).then_inc(sem["rstd_ready"], 1)

        @block.scalar
        def _(act):
            def copy_out(dst, src, func=ACT.Copy, **kw):
                return nc.scalar.activation(dst, src, func, **kw)

            act.wait_ge(sem["consts_loaded"], 96)
            nc.scalar.activation(tanhs[:, :], R[:, RTANH:RTANH + 4], ACT.Tanh).then_inc(sem["tanh_ready"], 1)
            nc.scalar.mul(xbq[:, 0:1], col("xq"), DK_SCALE)
            nc.scalar.mul(xbq[:, 1:2], col("fq"), DK_SCALE)
            nc.scalar.mul(xbq[:, 2:6], C[:, CSTACK:CSTACK + 4], DK_SCALE).then_inc(sem["tanh_ready"], 1)
            act.wait_ge(sem["tanh_ready"], 2)
            for n in range(2):
                act.wait_ge(sem["m_turn_psum"], n + 1)
                copy_out(M12[:, ts_(n, D)], bank(n, D, D)).then_inc(sem["m_ready"], 1)
            with act.Fori(0, GROUPS) as g:
                def turned(k, dst, **kw):
                    act.wait_ge(sem["tok_turned"], g * TURNS + k + 1)
                    copy_out(dst, bank(0, D, TG), **kw).then_inc(sem["tokT_ready"], 1)

                turned(0, HT[:, :])
                act.wait_ge(sem["r_psum"], 2 * g + 1)
                copy_out(RT[:, :], bank(1, D, TG)).then_inc(sem["rT_ready"], 1)
                act.wait_ge(sem["sm1_ready"], g + 1)
                for j in range(GROUP):
                    e = nc.scalar.activation(E1[:, j, :], E1[:, j, :], ACT.Exp, scale=DK_SCALE,
                                             bias=sm[:, 1, j:j + 1], accum_out=sm[:, 2, j:j + 1])
                e.then_inc(sem["e1_ready"], 1)
                act.wait_ge(sem["e1T_psum"], g + 1)
                copy_out(E1T[:, :], bank(5, T, TG)).then_inc(sem["e1T_ready"], 1)
                turned(1, HT[:, :])
                act.wait_ge(sem["r_psum"], 2 * g + 2)
                copy_out(RT[:, :], bank(1, D, TG)).then_inc(sem["rT_ready"], 1)
                for j in range(GROUP):
                    n = g * GROUP + j
                    act.wait_ge(sem["max2_ready"], n + 1)
                    if j:
                        act.wait_ge(sem["pT_psum"], n * 3)
                    nc.scalar.activation(PJ[0:T, :].rearrange("p (c k) -> p c k", c=3),
                                         psum[0:T, 3 * (j % 2):3 * (j % 2) + 3, 0:CHUNK], ACT.Exp,
                                         scale=DK_SCALE, bias=sm[:, 4, j:j + 1],
                                         accum_out=sm[:, 5, j:j + 1]).then_inc(sem["e2_ready"], 1)
                    for r in range(3):
                        act.wait_ge(sem["pT_psum"], n * 3 + r + 1)
                        if r == 0 and j:
                            act.wait_ge(sem["z2T_psum"], n)
                        if r < 2:
                            copy_out(PTA[:, 4 * r:4 * r + 4, :], bank(6, D, TG).rearrange("p (k t) -> p k t", k=4))\
                                .then_inc(sem["pT_ready"], 1)
                        else:
                            copy_out(PTA[:, 8:11, :], bank(6, D, 3 * T).rearrange("p (k t) -> p k t", k=3))
                            copy_out(PTA[0:REST, 11, :], bank(6, REST, T, 3 * T)).then_inc(sem["pT_ready"], 1)
                act.wait_ge(sem["z2T_psum"], g * GROUP + GROUP)
                copy_out(AT[:, :], bank(7, D, TG)).then_inc(sem["z2T_ready"], 1)
                turned(2, HT[:, :])
                act.wait_ge(sem["f1_psum"], g + 1)
                nc.scalar.activation(RT[:, :], bank(2, D, TG), ACT.Relu, bias=col("fc1")).then_inc(sem["f1_ready"], 1)
                turned(3, HQT[:, :])
                for j in range(GROUP):
                    n = g * GROUP + j
                    act.wait_ge(sem["gu_psum"], n + 1)
                    act.wait_ge(sem["factors_ready"], g + 1)
                    if j:
                        act.wait_ge(sem["aq_ready"], n)
                    nc.scalar.activation(EGT, bank(1 + 2 * (j % 2), T, INNER), ACT.Exp,
                                         scale=sm[:, 9, j:j + 1]).then_inc(sem["eg_ready"], 1)
                    act.wait_ge(sem["aqT_psum"], n + 1)
                    copy_out(AQT[:, :], bank(5, D, TG)).then_inc(sem["aqT_ready"], 1)
                turned(4, HT[:, :])
                act.wait_ge(sem["q_psum"], g + 1)
                nc.scalar.activation(AT[:, :], bank(1, D, TG), ACT.Identity, bias=xbq[:, 0:1],
                                     scale=DK_SCALE).then_inc(sem["q_ready"], 1)
                act.wait_ge(sem["qs_psum"], g + 1)
                for hg in range(HG):
                    e = nc.scalar.activation(T32[0:96, hg, :], bank(2 + hg, 96, TG), ACT.Identity,
                                             bias=xbq[0:96, 2 + hg:3 + hg], scale=DK_SCALE)
                e.then_inc(sem["qs_ready"], 1)
                for j in range(GROUP):
                    for kt in range(KT):
                        for a in range(2):
                            act.wait_ge(sem["st_psum"], (g * GROUP + j) * 2 * KT + 2 * kt + a + 1)
                            if a == 0 and (kt >= 2 or j):
                                act.wait_ge(sem["pv_done"], (g * GROUP + j) * KT + kt - 1)
                            nc.scalar.activation(PT[:, kt % 2, 2 * a:2 * a + 2, :], psum[:, 2 * a:2 * a + 2, 0:TG],
                                                 ACT.Exp).then_inc(sem["pt_ready"], 1)
                turned(5, HT[:, :])
                act.wait_ge(sem["fqk_psum"], g + 1)
                nc.scalar.activation(RT[:, :], bank(1, D, TG), ACT.Identity, bias=xbq[:, 1:2],
                                     scale=DK_SCALE).then_inc(sem["fq_ready"], 1)
                nc.scalar.activation(AT[:, :], bank(2, D, TG), ACT.Identity,
                                     bias=col("fk")).then_inc(sem["fk_ready"], 1)
                for j in range(GROUP):
                    n = g * GROUP + j
                    act.wait_ge(sem["fsub_ready"], n + 1)
                    nc.scalar.activation(SM2, SM2, ACT.Exp).then_inc(sem["fe_ready"], 1)
                    act.wait_ge(sem["feT_psum"], n + 1)
                    if j:
                        act.wait_ge(sem["fo_psum"], n)
                    copy_out(PT2.rearrange("p (b c) -> p b c", b=4), psum[0:T, 4:8, 0:TG]).then_inc(sem["feT_ready"], 1)
                turned(6, HT[:, :], func=ACT.Identity, bias=col("fv"))
                turned(7, HT[:, :])
                act.wait_ge(sem["gsub_ready"], g + 1)
                nc.scalar.activation(gt[:, 1, :], gt[:, 1, :], ACT.Exp).then_inc(sem["gexp_ready"], 1)
                act.wait_ge(sem["wT_psum"], g + 1)
                copy_out(WT[:, :], bank(3, EXPERTS, TG)).then_inc(sem["wT_ready"], 1)
                for e in range(EXPERTS):
                    for f in range(2):
                        n = 2 * e + f
                        act.wait_ge(sem["moe_h_psum"], g * FT + n + 1)
                        if e:
                            act.wait_ge(sem["moe_y_psum"], g * EXPERTS + e)
                        nc.scalar.activation(HE[:, f, :], bank(n % 4 + 1, D, TG), ACT.Relu,
                                             bias=C[:, CB1 + n:CB1 + n + 1]).then_inc(sem["moe_h_ready"], 1)

        @block.tensor
        def _(pe):
            mm = nc.tensor.matmul
            pe.wait_ge(sem["consts_loaded"], 96)
            for n, (a, b) in enumerate((("q1T", "k1T"), ("q2T", "k2T"))):
                mm(bank(n, D, D), w(a), w(b), start=True, stop=True).then_inc(sem["m_turn_psum"], 1)
            pe.wait_ge(sem["wsum_ready"], 1)
            pe.wait_ge(sem["ones_ready"], 1)
            mm(bank(2, D, 3), ones[:, :], wscale[:, 0:3], start=True, stop=True).then_inc(sem["wsum_psum"], 1)
            pe.wait_ge(sem["m_ready"], 2)
            pe.wait_ge(sem["wq_ready"], 1)
            pe.wait_ge(sem["cleared"], 1)
            pe.wait_ge(sem["big_loaded"], 48)
            with pe.Fori(0, GROUPS) as g:
                def turn(k, src):
                    pe.wait_ge(sem["tok_ready"], g * TURNS + k + 1)
                    for j in range(GROUP):
                        t = nc.tensor.transpose(bank(0, D, T, j * T), src[:, j, :], ident[0:T, 0:T])
                    t.then_inc(sem["tok_turned"], 1)
                    pe.wait_ge(sem["tokT_ready"], g * TURNS + k + 1)

                def per_seq(b, lhsT, rhs, sig, width=D):
                    for j in range(GROUP):
                        m = mm(bank(b, T, width, j * width), lhsT[:, ts_(j)], rhs, start=True, stop=True)
                    m.then_inc(sem[sig], 1)

                turn(0, H)
                mm(bank(1, D, TG), M12[:, 0:D], HT[:, :], start=True, stop=True).then_inc(sem["r_psum"], 1)
                per_seq(2, HT, w("v1"), "v1_psum")
                pe.wait_ge(sem["rT_ready"], 2 * g + 1)
                for j in range(GROUP):
                    m = mm(bank(3, T, T, j * T), RT[:, ts_(j)], HT[:, ts_(j)], start=True, stop=True)
                m.then_inc(sem["s1_psum"], 1)
                pe.wait_ge(sem["len1_ready"], g + 1)
                mm(bank(4, T, GROUP), ones[0:1, 0:T], len1[:, :], start=True, stop=True).then_inc(sem["len1_psum"], 1)
                pe.wait_ge(sem["e1_ready"], g + 1)
                for j in range(GROUP):
                    m = nc.tensor.transpose(bank(5, T, T, j * T), E1[:, j, :], ident[0:T, 0:T])
                m.then_inc(sem["e1T_psum"], 1)
                pe.wait_ge(sem["e1T_ready"], g + 1)
                pe.wait_ge(sem["v1_ready"], g + 1)
                for j in range(GROUP):
                    m = mm(bank(6, T, D, j * D), E1T[:, ts_(j)], VS[:, j, :], start=True, stop=True)
                m.then_inc(sem["z1_psum"], 1)
                turn(1, Y)
                mm(bank(1, D, TG), M12[:, D:2 * D], HT[:, :], start=True, stop=True).then_inc(sem["r_psum"], 1)
                pe.wait_ge(sem["rT_ready"], 2 * g + 2)

                def scores(j):
                    n = g * GROUP + j
                    pe.wait_ge(ct_loaded[j % 2], (4 * g + j // 2 + 1) * 16)
                    if j >= 2:
                        pe.wait_ge(sem["e2_ready"], n - 1)
                    for c in range(3):
                        m = mm(bank(3 * (j % 2) + c, T, CHUNK), RT[:, ts_(j)],
                               CT[:, j % 2, c * CHUNK:(c + 1) * CHUNK], start=True, stop=True)
                    m.then_inc(sem["s2_psum"], 1)
                    pe.wait_ge(sem["row_ready"], n + 1)
                    for c in range(3):
                        m = mm(bank(3 * (j % 2) + c, T, CHUNK), cut_row[:, 0:T],
                               prow[:, c * CHUNK:(c + 1) * CHUNK], start=False, stop=True, skip_group_check=True)
                    m.then_inc(sem["s2m_psum"], 1)

                def values(j):
                    n = g * GROUP + j
                    pe.wait_ge(sem["e2_ready"], n + 1)
                    pe.wait_ge(cn_loaded[j % 2], (2 * g + j // 2 + 1) * 32)
                    for r in range(3):
                        if r:
                            pe.wait_ge(sem["pT_ready"], n * 3 + r)
                        elif j:
                            pe.wait_ge(sem["pT_ready"], n * 3)
                        for k in range(4 * r, 4 * r + 4):
                            rows = D if k < KT - 1 else REST
                            m = nc.tensor.transpose(bank(6, rows, T, (k % 4) * T), PJ[0:T, k * D:k * D + rows],
                                                    ident[0:T, 0:T])
                        m.then_inc(sem["pT_psum"], 1)
                    pe.wait_ge(sem["pT_ready"], n * 3 + 3)
                    for k in range(KT):
                        rows = D if k < KT - 1 else REST
                        m = mm(bank(7, D, T, j * T), CN[0:rows, j % 2, k, :], PTA[0:rows, k, :],
                               start=(k == 0), stop=(k == KT - 1))
                    m.then_inc(sem["z2T_psum"], 1)

                scores(0)
                for j in range(GROUP):
                    if j + 1 < GROUP:
                        scores(j + 1)
                    values(j)
                pe.wait_ge(sem["z2T_ready"], g + 1)
                per_seq(0, AT, w("v2"), "z2_psum")
                turn(2, Y)
                mm(bank(2, D, TG), w("fc1"), HT[:, :], start=True, stop=True).then_inc(sem["f1_psum"], 1)
                pe.wait_ge(sem["f1_ready"], g + 1)
                per_seq(3, RT, w("fc2"), "f2_psum")
                turn(3, U)

                def gate_up(j):
                    if j >= 2:
                        pe.wait_ge(sem["gu_used"], g * GROUP + j - 1)
                    b = 1 + 2 * (j % 2)
                    mm(bank(b, T), HQT[:, ts_(j)], wq_int[:, 0:INNER], start=True, stop=True)
                    mm(bank(b + 1, T), HQT[:, ts_(j)], wq_int[:, INNER:2 * INNER], start=True, stop=True)\
                        .then_inc(sem["gu_psum"], 1)

                gate_up(0)
                gate_up(1)
                for j in range(GROUP):
                    n = g * GROUP + j
                    pe.wait_ge(sem["aq_ready"], n + 1)
                    for c in range(4):
                        m = nc.tensor.transpose(bank(5, D, T, c * T), AQ[:, c * D:(c + 1) * D], ident[0:T, 0:T])
                    m.then_inc(sem["aqT_psum"], 1)
                    pe.wait_ge(sem["aqT_ready"], n + 1)
                    for c in range(4):
                        m = mm(bank(6, T, D, j * D), AQT[:, ts_(c)],
                               wq_int[:, 2 * INNER + c * D:2 * INNER + (c + 1) * D], start=(c == 0), stop=(c == 3))
                    m.then_inc(sem["down_psum"], 1)
                    if j + 2 < GROUP:
                        gate_up(j + 2)
                turn(4, H)
                mm(bank(1, D, TG), w("xqT"), HT[:, :], start=True, stop=True).then_inc(sem["q_psum"], 1)
                for hg in range(HG):
                    m = mm(bank(2 + hg, 96, TG), W[:, WSTACK + 96 * hg:WSTACK + 96 * hg + 96], HT[:, :],
                           start=True, stop=True)
                m.then_inc(sem["qs_psum"], 1)
                pe.wait_ge(sem["q_ready"], g + 1)
                pe.wait_ge(sem["qs_ready"], g + 1)

                def job(j, n):
                    at = (g * GROUP + j) * JOBS + n
                    b = 4 + n % 2
                    if j or n >= 2:
                        pe.wait_ge(sem["ring_drained"], at - 1)
                    if n == 0:
                        pe.wait_ge(ct_loaded[j % 2], (4 * g + 2 + j // 2 + 1) * 16)
                    if n < 3:
                        c, size = CHUNKS[n]
                        m = mm(bank(b, D, size), w("xkT"), CT[:, j % 2, c:c + size], start=True, stop=True)
                    elif n < 6:
                        for k in range(4 * (n - 3), 4 * (n - 3) + 4):
                            rows = D if k < KT - 1 else REST
                            m = mm(bank(b, rows, D, (k % 4) * D), CT[:, j % 2, k * D:k * D + rows], w("xvT"),
                                   start=True, stop=True)
                    elif n < JOBS - 1:
                        q, i = divmod(n - 6, 3)
                        if n == 6:
                            pe.wait_ge(sem["kh_ready"], g * GROUP + j + 1)
                            pe.wait_ge(sem["qbd_ready"], g * GROUP + j + 1)
                        c, size = CHUNKS[i]
                        m = mm(bank(b, D, size), QBD[:, q * D:(q + 1) * D], KH[:, c:c + size], start=True, stop=True)
                    else:
                        pe.wait_ge(sem["mx_ready"], g * GROUP + j + 1)
                        m = nc.tensor.transpose(bank(b, QCH, D), mx[:, 0:QCH], ident)
                    m.then_inc(sem["ring_filled"], 1)

                def score_half(j, kt, a):
                    at = (g * GROUP + j) * 2 * KT + 2 * kt + a
                    if kt == 0 and a == 0:
                        pe.wait_ge(ks_loaded[j % 2], (2 * g + j // 2 + 1) * 16 * KS_DMAS)
                        pe.wait_ge(qrow_loaded[j % 2], (2 * g + j // 2 + 1) * 32)
                        pe.wait_ge(sem["qexp_ready"], g * GROUP + j + 1)
                    if j or kt:
                        pe.wait_ge(sem["pt_ready"], at - 1)
                    for hg in (2 * a, 2 * a + 1):
                        m = mm(bank(hg, D, TG), KS[0:STACK, j % 2, hg, kt * D:(kt + 1) * D],
                               QS[0:STACK, j % 2, hg * TG:(hg + 1) * TG], start=True, stop=True)
                    m.then_inc(sem["st_psum"], 1)

                def weigh(j, kt):
                    pe.wait_ge(sem["pt_ready"], (g * GROUP + j) * 2 * KT + 2 * kt + 2)
                    if kt == 0 and j:
                        pe.wait_ge(sem["att_free"], g * GROUP + j)
                    count = ones[:, 0:32] if kt < KT - 1 else K[:, K_LAST:K_LAST + 32]
                    for b in (6, 7):
                        for hg in range(HG):
                            left = V[:, j % 2, kt, 32 * hg:32 * hg + 32] if b == 6 else count
                            m = mm(psum[32 * hg:32 * hg + 32, b, 0:TG], left, PT[:, kt % 2, hg, :],
                                   start=(kt == 0), stop=(kt == KT - 1), tile_position=(0, 32 * hg))
                    m.then_inc(sem["pv_done"], 1)

                for n in range(JOBS):
                    job(0, n)
                for j in range(GROUP):
                    todo = list(range(JOBS)) if j + 1 < GROUP else []
                    score_half(j, 0, 0)
                    score_half(j, 0, 1)
                    for kt in range(KT):
                        if kt + 1 < KT:
                            score_half(j, kt + 1, 0)
                        for n in todo[4 * kt:4 * kt + 2]:
                            job(j + 1, n)
                        if kt + 1 < KT:
                            score_half(j, kt + 1, 1)
                        weigh(j, kt)
                        for n in todo[4 * kt + 2:4 * kt + 4]:
                            job(j + 1, n)
                pe.wait_ge(sem["att_ready"], g * GROUP + GROUP)
                per_seq(4, AT, w("xoT"), "attx_psum")
                turn(5, H)
                mm(bank(1, D, TG), w("fq"), HT[:, :], start=True, stop=True)
                mm(bank(2, D, TG), w("fk"), HT[:, :], start=True, stop=True).then_inc(sem["fqk_psum"], 1)
                per_seq(3, HT, w("fv"), "fv_psum")
                pe.wait_ge(sem["fq_ready"], g + 1)
                pe.wait_ge(sem["fv_ready"], g + 1)
                for j in range(GROUP):
                    n = g * GROUP + j
                    pe.wait_ge(sem["kbd_ready"], n + 1)
                    if j:
                        pe.wait_ge(sem["feT_ready"], n)
                    for c in range(4):
                        m = mm(bank(4 + c, T, TG), RT[:, ts_(j)], KBD[:, c * TG:(c + 1) * TG], start=True, stop=True)
                    m.then_inc(sem["fs_psum"], 1)
                    pe.wait_ge(sem["fe_ready"], n + 1)
                    for h in range(HEADS):
                        m = nc.tensor.transpose(bank(4 + h // 4, T, T, (h % 4) * T), SM2[:, h * T:(h + 1) * T],
                                                ident[0:T, 0:T])
                    m.then_inc(sem["feT_psum"], 1)
                    pe.wait_ge(sem["feT_ready"], n + 1)
                    for h in range(HEADS):
                        m = mm(bank(3, T, HD, j * D + h * HD), PT2[:, h * T:(h + 1) * T],
                               VS[:, j, h * HD:(h + 1) * HD], start=True, stop=True)
                    m.then_inc(sem["fo_psum"], 1)
                turn(6, U)
                per_seq(1, HT, w("fo"), "wo_psum")
                turn(7, Y)
                per_seq(2, HT, W[:, WGATE:WGATE + EXPERTS], "gate_psum", EXPERTS)
                pe.wait_ge(sem["w_ready"], g + 1)
                for j in range(GROUP):
                    m = nc.tensor.transpose(bank(3, EXPERTS, T, j * T), gt[:, 2, j * EXPERTS:(j + 1) * EXPERTS],
                                            ident[0:T, 0:T])
                m.then_inc(sem["wT_psum"], 1)
                pe.wait_ge(sem["wT_ready"], g + 1)
                per_seq(4, WT, B2[:, :], "b2_psum")
                pe.wait_ge(sem["moe_y_used"], (EXPERTS + 1) * g + 1)

                def hidden(e):
                    for f in range(2):
                        n = 2 * e + f
                        if e >= 2:
                            pe.wait_ge(sem["moe_h_ready"], g * FT + n - 3)
                        mm(bank(n % 4 + 1, D, TG), W1[:, n * D:(n + 1) * D], HT[:, :],
                           start=True, stop=True).then_inc(sem["moe_h_psum"], 1)

                hidden(0)
                for e in range(EXPERTS):
                    if e + 1 < EXPERTS:
                        hidden(e + 1)
                    pe.wait_ge(sem["moe_h_ready"], g * FT + 2 * e + 2)
                    if e >= 2:
                        pe.wait_ge(sem["moe_y_used"], (EXPERTS + 1) * g + e)
                    for j in range(GROUP):
                        for f in range(2):
                            n = 2 * e + f
                            m = mm(bank(5 + e % 2, T, D, j * D), HE[:, f, ts_(j)], W2[:, n * D:(n + 1) * D],
                                   start=(f == 0), stop=(f == 1))
                    m.then_inc(sem["moe_y_psum"], 1)

        @block.vector
        def _(dve):
            v = nc.vector
            state = {"n": 0, "base": 0}

            def link(ins, plain=False):
                state["n"] += 1
                ins.then_inc(dve_chain, 1)
                dve.wait_ge(dve_chain, state["base"] + state["n"])
                if plain:
                    v.memset(carrier[:, :], 0.0)

            def ts(*a, **k):
                return v.tensor_scalar(*a, **k)

            dve.wait_ge(sem["consts_loaded"], 96)
            dve.wait_ge(sem["cleared"], 1)
            wv = WRAW.rearrange("p (m c) -> p m c", m=3)
            v.tensor_reduce(wscale[:, 0:3], wv, AX.X, ALU.add, apply_absolute_value=True).then_inc(sem["wsum_ready"], 1)
            dve.wait_ge(sem["wsum_psum"], 1)
            link(ts(wscale[:, 3:6], bank(2, D, 3), 1.0 / (D * INNER), 1e-5, ALU.mult, ALU.max))
            link(v.reciprocal(wscale[:, 6:9], wscale[:, 3:6]))
            for m in range(3):
                last = ts(WTMP[:, m * INNER:(m + 1) * INNER], WRAW[:, m * INNER:(m + 1) * INNER],
                          wscale[:, 6 + m:7 + m], ROUND, ALU.mult, ALU.add)
            link(last)
            link(ts(WTMP, WTMP, -ROUND, 1.0, ALU.add, ALU.min))
            link(ts(wq_int[:, :], WTMP, -1.0, None, ALU.max))
            link(v.tensor_copy(PEN, MB[0:BATCH, 0, :]))
            link(v.tensor_reduce(mx[0:BATCH, 15:16], PEN, AX.X, ALU.max))
            link(ts(mx[0:BATCH, 15:16], mx[0:BATCH, 15:16], PENALTY, None, ALU.mult))
            ts(PENR, PEN, -1.0, mx[0:BATCH, 15:16], ALU.add, ALU.mult).then_inc(sem["pen_ready0"], 1)
            dve.wait_ge(sem["pen_stored"], 16)
            ts(len2[:, :], wscale[0:1, 3:4], 1.0, None, ALU.mult).then_inc(sem["wq_ready"], 1)
            dve.wait_ge(sem["wq_ready"], 1)
            v.memset(carrier[:, :], 0.0).then_inc(sem["out_ready"], 1)
            dve.wait_ge(sem["out_ready"], 1)
            dve.wait_ge(sem["tanh_ready"], 2)
            setup_links = state["n"]

            with dve.Fori(0, GROUPS) as g:
                state["n"] = 0
                state["base"] = g * DVE_LINKS + setup_links

                def tok_done(ins, k):
                    ins.then_inc(sem["tok_ready"], 1)
                    dve.wait_ge(sem["tok_ready"], g * TURNS + k + 1)

                def norm(k, src, dst, gain=None):
                    for j in range(GROUP):
                        last = v.bn_stats(st[:, j, :], src[:, j, :])
                    link(last, plain=True)
                    for j in range(GROUP):
                        last = v.bn_aggr(mv[:, j, :], st[:, j, :])
                    link(last)
                    ts(ve[:, :], mv[:, :, 1], EPS, None, ALU.add).then_inc(sem["var_ready"], 1)
                    dve.wait_ge(sem["rstd_ready"], g * LNS + k + 1)
                    for j in range(GROUP):
                        last = ts(dst[:, j, :], src[:, j, :], mv[:, j, 0:1], rs[:, j:j + 1], ALU.subtract, ALU.mult)
                    if gain is None:
                        return last
                    link(last)
                    link(v.tensor_tensor(dst[:, :, :], dst[:, :, :], row(gain + "g"), ALU.mult))
                    return v.tensor_tensor(dst[:, :, :], dst[:, :, :], row(gain + "b"), ALU.add)

                def quantise(src, dst, amax, scale, rows=T):
                    n = amax.shape[1]
                    link(v.tensor_reduce(amax, src, AX.X, ALU.max, apply_absolute_value=True))
                    link(ts(amax, amax, 1e-5, None, ALU.max))
                    link(v.reciprocal(scale, amax))
                    link(ts(scale, scale, 127.0, None, ALU.mult))
                    for j in range(n):
                        s = src[:, j, :] if n > 1 else src
                        d = dst[:, j, :] if n > 1 else dst
                        last = ts(d, s, scale[:, j:j + 1], ROUND, ALU.mult, ALU.add)
                    link(last)
                    link(ts(dst, dst, -ROUND, 127.0, ALU.add, ALU.min))
                    return ts(dst, dst, -128.0, None, ALU.max)

                dve.wait_ge(sem["x_loaded"], (g + 1) * 16)
                tok_done(norm(0, X, H), 0)
                dve.wait_ge(sem["v1_psum"], g + 1)
                v.tensor_copy(VS[:, :, :], tok_bank(2)).then_inc(sem["v1_ready"], 1)
                dve.wait_ge(sem["s1_psum"], g + 1)
                s1 = psum[0:T, 3, 0:TG].rearrange("p (j k) -> p j k", j=GROUP)
                link(ts(E1[0:1, :, :], s1[0:1, :, :], 0.0, None, ALU.not_equal))
                v.tensor_reduce(len1[:, :], E1[0:1, :, :], AX.X, ALU.add).then_inc(sem["len1_ready"], 1)
                dve.wait_ge(sem["len1_psum"], g + 1)
                link(v.tensor_copy(sm[:, 3, :], bank(4, T, GROUP)))
                base = K[0:T, K_BASE:K_BASE + T].unsqueeze(1).to_broadcast([T, GROUP, T])
                link(v.tensor_tensor(E1[:, :, :], base, sm[:, 3, :].unsqueeze(2).to_broadcast([T, GROUP, T]), ALU.add))
                link(ts(E1[:, :, :], E1[:, :, :], 0.0, CUT, ALU.min, ALU.mult))
                link(v.tensor_tensor(E1[:, :, :], s1, E1[:, :, :], ALU.add))
                link(v.tensor_reduce(sm[:, 0, :], E1[:, :, :], AX.X, ALU.max))
                ts(sm[:, 1, :], sm[:, 0, :], -DK_SCALE, None, ALU.mult).then_inc(sem["sm1_ready"], 1)
                dve.wait_ge(sem["e1_ready"], g + 1)
                link(v.reciprocal(sm[:, 2, :], sm[:, 2, :]))
                dve.wait_ge(sem["z1_psum"], g + 1)
                for j in range(GROUP):
                    last = v.scalar_tensor_tensor(out=U[:, j, :], in0=tok_bank(6)[:, j, :], scalar=sm[:, 2, j:j + 1],
                                                  in1=H[:, j, :], op0=ALU.mult, op1=ALU.add)
                link(last)
                tok_done(norm(1, U, Y, "ln1"), 1)
                for j in range(GROUP):
                    n = g * GROUP + j
                    sc = psum[0:T, 3 * (j % 2):3 * (j % 2) + 3, 0:CHUNK]
                    dve.wait_ge(sem["s2_psum"], n + 1)
                    link(ts(PT[0:1, 0, :, :].rearrange("p a b -> p (a b)")[:, 0:SPAD].rearrange("p (c k) -> p c k", c=3),
                            sc[0:1, :, :], 0.0, None, ALU.not_equal, ALU.add, accum_out=len2[:, :]))
                    if j:
                        dve.wait_ge(sem["s2m_psum"], n)
                    link(ts(PT[0:1, 1, :, :].rearrange("p a b -> p (a b)")[:, 0:SPAD], key_row[:, :], len2[:, :], -0.5,
                            ALU.add, ALU.add))
                    ts(prow[:, :], PT[0:1, 1, :, :].rearrange("p a b -> p (a b)")[:, 0:SPAD], 0.0, None, ALU.min)\
                        .then_inc(sem["row_ready"], 1)
                    dve.wait_ge(sem["s2m_psum"], n + 1)
                    link(v.tensor_reduce(sm[:, 6, j:j + 1], sc, AX.XY, ALU.max))
                    ts(sm[:, 4, j:j + 1], sm[:, 6, j:j + 1], -DK_SCALE, None, ALU.mult).then_inc(sem["max2_ready"], 1)
                dve.wait_ge(sem["e2_ready"], g * GROUP + GROUP)
                link(v.reciprocal(sm[:, 5, :], sm[:, 5, :]))
                dve.wait_ge(sem["z2_psum"], g + 1)
                for j in range(GROUP):
                    last = v.scalar_tensor_tensor(out=U[:, j, :], in0=tok_bank(0)[:, j, :], scalar=sm[:, 5, j:j + 1],
                                                  in1=Y[:, j, :], op0=ALU.mult, op1=ALU.add)
                link(last)
                tok_done(norm(2, U, Y, "ln2"), 2)
                dve.wait_ge(sem["f2_psum"], g + 1)
                link(v.tensor_tensor(U[:, :, :], tok_bank(3), row("fc2b"), ALU.add))
                link(v.tensor_tensor(U[:, :, :], U[:, :, :], Y[:, :, :], ALU.add))
                link(norm(3, U, Y, "ln3"))
                link(v.scalar_tensor_tensor(out=X[:, :, :], in0=Y[:, :, :], scalar=tanhs[:, 0:1], in1=X[:, :, :],
                                            op0=ALU.mult, op1=ALU.add))
                link(norm(4, X, H))
                tok_done(quantise(H[:, :, :], U[:, :, :], sm[:, 7, :], sm[:, 8, :]), 3)
                ts(sm[:, 9, :], sm[:, 7, :], wscale[0:T, 3:4], -1.0 / 127.0, ALU.mult, ALU.mult)
                ts(sm[:, 10, :], sm[:, 7, :], wscale[0:T, 3:4], 1.0 / 127.0, ALU.mult, ALU.mult)
                link(ts(sm[:, 11, :], sm[:, 7, :], wscale[0:T, 4:5], 1.0 / 127.0, ALU.mult, ALU.mult))
                link(ts(sm[:, 12, 0:1], wscale[0:T, 5:6], tanhs[:, 2:3], None, ALU.mult))
                ts(sm[:, 12, 0:1], sm[:, 12, 0:1], 1.0 / 127.0, None, ALU.mult).then_inc(sem["factors_ready"], 1)
                dve.wait_ge(sem["factors_ready"], g + 1)
                for j in range(GROUP):
                    n = g * GROUP + j
                    b = 1 + 2 * (j % 2)
                    dve.wait_ge(sem["eg_ready"], n + 1)
                    link(ts(EGT, EGT, 1.0, None, ALU.add))
                    link(v.reciprocal(EGT, EGT))
                    link(v.scalar_tensor_tensor(out=EGT, in0=bank(b, T), scalar=sm[:, 10, j:j + 1], in1=EGT,
                                                op0=ALU.mult, op1=ALU.mult))
                    v.scalar_tensor_tensor(out=EGT, in0=bank(b + 1, T), scalar=sm[:, 11, j:j + 1], in1=EGT,
                                           op0=ALU.mult, op1=ALU.mult).then_inc(sem["gu_used"], 1)
                    dve.wait_ge(sem["gu_used"], n + 1)
                    if j:
                        dve.wait_ge(sem["aqT_psum"], n)
                    quantise(EGT, AQ, sm[:, 13, j:j + 1], sm[:, 14, j:j + 1]).then_inc(sem["aq_ready"], 1)
                    link(ts(sm[:, 15, j:j + 1], sm[:, 13, j:j + 1], sm[:, 12, 0:1], None, ALU.mult))
                dve.wait_ge(sem["down_psum"], g * GROUP + GROUP)
                for j in range(GROUP):
                    last = v.scalar_tensor_tensor(out=X[:, j, :], in0=tok_bank(6)[:, j, :], scalar=sm[:, 15, j:j + 1],
                                                  in1=X[:, j, :], op0=ALU.mult, op1=ALU.add)
                link(last)
                tok_done(norm(5, X, H), 4)
                dve.wait_ge(sem["qs_ready"], g + 1)
                hi = KL[0:96, :].rearrange("p (a b) -> p a b", a=HG)
                link(v.tensor_copy(hi, T32[0:96, :, :]))
                link(v.scalar_tensor_tensor(out=QR[:, :, :], in0=hi.bitcast(F32), scalar=K[0:96, K_NEG1:K_NEG1 + 1],
                                            in1=T32[0:96, :, :], op0=ALU.mult, op1=ALU.add))
                dve.wait_ge(sem["q_ready"], g + 1)

                def prepare(j):
                    n = g * GROUP + j
                    p = j % 2
                    if j:
                        pass
                    v.tensor_tensor(QBD[:, 0:HQ].rearrange("p (h q) -> p h q", h=HEADS),
                                    AT_q(j), mask16.unsqueeze(2).to_broadcast([D, HEADS, T]),
                                    ALU.mult).then_inc(sem["qbd_ready"], 1)
                    if j >= 2:
                        dve.wait_ge(sem["pv_done"], (n - 1) * KT)
                    for hg in range(HG):
                        last = v.tensor_tensor(QS[0:96, p, hg * TG:(hg + 1) * TG].rearrange("p (h q) -> p h q", h=HG),
                                               QR[:, hg, ts_(j)].unsqueeze(1).to_broadcast([96, HG, T]),
                                               K[0:96, K_M4:K_M4 + HG].unsqueeze(2).to_broadcast([96, HG, T]), ALU.mult)
                    last.then_inc(sem["qexp_ready"], 1)
                    if j < 2:
                        dve.wait_ge(sem["z2T_psum"], g * GROUP + GROUP)
                        v.memset(V[:, p, KT - 1, :], 0.0)
                    dve.wait_ge(mask_loaded[p], (2 * g + j // 2 + 1) * 16)
                    for i, (c, size) in enumerate(CHUNKS):
                        dve.wait_ge(sem["ring_filled"], n * JOBS + i + 1)
                        v.scalar_tensor_tensor(out=KT32[:, c:c + size], in0=bank(4 + i % 2, D, size), scalar=col("xk"),
                                               in1=MB[:, p, c:c + size], op0=ALU.add, op1=ALU.mult)\
                            .then_inc(sem["ring_drained"], 1)
                    dve.wait_ge(sem["ring_drained"], n * JOBS + 3)
                    if j:
                        q = j - 1
                        dve.wait_ge(ks_loaded[q % 2], (2 * g + q // 2 + 1) * 16 * KS_DMAS)
                    v.tensor_copy(KH[:, :], KT32[:, 0:S]).then_inc(sem["kh_ready"], 1)
                    dve.wait_ge(sem["kh_ready"], n + 1)
                    v.tensor_tensor(KL[:, 0:S], KT32[:, 0:S], KH[:, :].bitcast(F32), ALU.subtract)\
                        .then_inc(sem["kl_ready"], 1)
                    for i in range(3, 6):
                        dve.wait_ge(sem["ring_filled"], n * JOBS + i + 1)
                        if i < 5:
                            v.tensor_copy(V[:, p, 4 * (i - 3):4 * (i - 3) + 4, :],
                                          bank(4 + i % 2).rearrange("p (k d) -> p k d", k=4)).then_inc(sem["ring_drained"], 1)
                        else:
                            v.tensor_copy(V[:, p, 8:11, :], bank(4 + i % 2, D, 3 * D).rearrange("p (k d) -> p k d", k=3))
                            v.tensor_copy(V[0:REST, p, 11, :], bank(4 + i % 2, REST, D, 3 * D)).then_inc(sem["ring_drained"], 1)
                    for i in range(6, JOBS - 1):
                        q, c = divmod(i - 6, 3)
                        dve.wait_ge(sem["ring_filled"], n * JOBS + i + 1)
                        v.tensor_reduce(KT32[:, 0:48].rearrange("p (q c) -> p q c", c=3)[:, q, c:c + 1],
                                        bank(4 + i % 2, D, CHUNKS[c][1]), AX.X, ALU.max).then_inc(sem["ring_drained"], 1)
                    dve.wait_ge(sem["ring_drained"], n * JOBS + JOBS - 1)
                    v.tensor_reduce(mx[:, 0:QCH], KT32[:, 0:3 * QCH].rearrange("p (q c) -> p q c", c=3), AX.X, ALU.max,
                                    negate=True).then_inc(sem["mx_ready"], 1)
                    dve.wait_ge(sem["ring_filled"], (n + 1) * JOBS)
                    if j:
                        q = j - 1
                        dve.wait_ge(qrow_loaded[q % 2], (2 * g + q // 2 + 1) * 32)
                    link(v.tensor_copy(NMH[:, :], bank(4 + (JOBS - 1) % 2, QCH, D)))
                    v.tensor_tensor(NML[:, :], bank(4 + (JOBS - 1) % 2, QCH, D), NMH[:, :].bitcast(F32),
                                    ALU.subtract).then_inc(sem["nm_ready"], 1)
                    dve.wait_ge(sem["nm_ready"], n + 1)
                    v.tensor_copy(mx[0:1, 14:15], mx[0:1, 14:15]).then_inc(sem["ring_drained"], 1)

                def AT_q(j):
                    return AT[:, ts_(j)].unsqueeze(1).to_broadcast([D, HEADS, T])

                def attend(j):
                    n = g * GROUP + j
                    dve.wait_ge(sem["pv_done"], (n + 1) * KT)
                    def b4(b):
                        return psum[:, b, 0:TG].rearrange("p (h q) -> p h q", h=HG)
                    link(v.reciprocal(sm4[:, :, :], b4(7)))
                    v.tensor_tensor(sm4[:, :, :], b4(6), sm4[:, :, :], ALU.mult).then_inc(sem["att_free"], 1)
                    dve.wait_ge(sem["att_free"], n + 1)
                    link(v.tensor_tensor(sm4[:, :, :], sm4[:, :, :], mask4.unsqueeze(2).to_broadcast([D, HG, T]), ALU.mult))
                    link(v.tensor_reduce(AT[:, ts_(j)], sm4[:, :, :].rearrange("p h q -> p q h"), AX.X, ALU.add))
                    ts(AT[:, ts_(j)], AT[:, ts_(j)], col("xv"), None, ALU.add).then_inc(sem["att_ready"], 1)

                prepare(0)
                for j in range(GROUP):
                    if j + 1 < GROUP:
                        prepare(j + 1)
                    attend(j)
                dve.wait_ge(sem["attx_psum"], g + 1)
                link(v.tensor_tensor(U[:, :, :], tok_bank(4), row("xbo"), ALU.add))
                link(v.scalar_tensor_tensor(out=X[:, :, :], in0=U[:, :, :], scalar=tanhs[:, 1:2], in1=X[:, :, :],
                                            op0=ALU.mult, op1=ALU.add))
                tok_done(norm(6, X, H), 5)
                dve.wait_ge(sem["fv_psum"], g + 1)
                v.tensor_copy(VS[:, :, :], tok_bank(3)).then_inc(sem["fv_ready"], 1)
                dve.wait_ge(sem["fk_ready"], g + 1)
                for j in range(GROUP):
                    n = g * GROUP + j
                    sc = psum[0:T, 4:8, 0:TG].rearrange("p b (h k) -> p b h k", h=4)
                    s2 = SM2.rearrange("p (b h k) -> p b h k", b=4, h=4)
                    if j:
                        dve.wait_ge(sem["fs_psum"], n)
                    v.tensor_tensor(KBD.rearrange("p (h k) -> p h k", h=HEADS),
                                    AT_q(j), mask16.unsqueeze(2).to_broadcast([D, HEADS, T]),
                                    ALU.mult).then_inc(sem["kbd_ready"], 1)
                    dve.wait_ge(sem["fs_psum"], n + 1)
                    link(v.tensor_reduce(dn[:, 0, :], sc, AX.X, ALU.max))
                    for c in range(4):
                        last = v.tensor_tensor(s2[:, c, :, :], sc[:, c, :, :],
                                               dn[:, 0, 4 * c:4 * c + 4].unsqueeze(2).to_broadcast([T, 4, T]), ALU.subtract)
                    last.then_inc(sem["fsub_ready"], 1)
                    dve.wait_ge(sem["fe_ready"], n + 1)
                    link(v.tensor_reduce(dn[:, 1, :], SM2.rearrange("p (h k) -> p h k", h=HEADS), AX.X, ALU.add))
                    link(v.reciprocal(dn[:, 1, :], dn[:, 1, :]))
                    dve.wait_ge(sem["fo_psum"], n + 1)
                    last = v.tensor_tensor(U[:, j, :].rearrange("p (h d) -> p h d", h=HEADS),
                                           tok_bank(3)[:, j, :].rearrange("p (h d) -> p h d", h=HEADS),
                                           dn[:, 1, :].unsqueeze(2).to_broadcast([T, HEADS, HD]), ALU.mult)
                    if j < GROUP - 1:
                        link(last)
                tok_done(last, 6)
                dve.wait_ge(sem["wo_psum"], g + 1)
                link(v.tensor_tensor(U[:, :, :], tok_bank(1), row("fbo"), ALU.add))
                link(v.tensor_tensor(U[:, :, :], U[:, :, :], H[:, :, :], ALU.add))
                tok_done(norm(7, U, Y, "fln1"), 7)
                def ge(i):
                    return gt[:, i, :].rearrange("p (j e) -> p j e", j=GROUP)

                def gj(i, j):
                    return gt[:, i, j * EXPERTS:(j + 1) * EXPERTS]
                wide = [T, GROUP, EXPERTS]
                dve.wait_ge(sem["gate_psum"], g + 1)
                link(v.tensor_tensor(ge(0), psum[0:T, 2, 0:GROUP * EXPERTS].rearrange("p (j e) -> p j e", j=GROUP),
                                     R[:, RGB:RGB + EXPERTS].unsqueeze(1).to_broadcast(wide), ALU.add))
                link(v.tensor_reduce(sm[:, 0, :], ge(0), AX.X, ALU.max))
                v.tensor_tensor(ge(1), ge(0), sm[:, 0, :].unsqueeze(2).to_broadcast(wide), ALU.subtract)\
                    .then_inc(sem["gsub_ready"], 1)
                dve.wait_ge(sem["gexp_ready"], g + 1)
                link(v.tensor_reduce(sm[:, 1, :], ge(1), AX.X, ALU.add))
                link(v.reciprocal(sm[:, 1, :], sm[:, 1, :]))
                link(v.tensor_tensor(ge(0), ge(1), sm[:, 1, :].unsqueeze(2).to_broadcast(wide), ALU.mult), plain=True)
                for j in range(GROUP):
                    last = v.max(gj(3, j), gj(0, j))
                link(last, plain=True)
                for j in range(GROUP):
                    last = v.max_index(gi[:, j * EXPERTS:(j + 1) * EXPERTS], gj(3, j), gj(0, j))
                link(last)
                link(v.tensor_copy(gt[:, 4, :], gi[:, :]))
                iota8 = K[0:T, K_IOTA:K_IOTA + EXPERTS]
                for j in range(GROUP):
                    for n, dst in ((0, 2), (1, 5)):
                        last = ts(gj(dst, j), iota8, gj(4, j)[:, n:n + 1], gj(3, j)[:, n:n + 1], ALU.is_equal, ALU.mult)
                link(last)
                v.tensor_tensor(gt[:, 2, :], gt[:, 2, :], gt[:, 5, :], ALU.add).then_inc(sem["w_ready"], 1)
                dve.wait_ge(sem["w_ready"], g + 1)
                dve.wait_ge(sem["b2_psum"], g + 1)
                v.tensor_tensor(U[:, :, :], tok_bank(4), Y[:, :, :], ALU.add).then_inc(sem["moe_y_used"], 1)
                for e in range(EXPERTS):
                    dve.wait_ge(sem["moe_y_used"], (EXPERTS + 1) * g + e + 1)
                    dve.wait_ge(sem["moe_y_psum"], g * EXPERTS + e + 1)
                    for j in range(GROUP):
                        last = v.scalar_tensor_tensor(out=U[:, j, :], in0=tok_bank(5 + e % 2)[:, j, :],
                                                      scalar=gj(2, j)[:, e:e + 1], in1=U[:, j, :],
                                                      op0=ALU.mult, op1=ALU.add)
                    last.then_inc(sem["moe_y_used"], 1)
                dve.wait_ge(sem["moe_y_used"], (EXPERTS + 1) * (g + 1))
                link(norm(8, U, H, "fln2"))
                v.scalar_tensor_tensor(out=Y[:, :, :], in0=H[:, :, :], scalar=tanhs[:, 3:4], in1=X[:, :, :],
                                       op0=ALU.mult, op1=ALU.add).then_inc(sem["out_ready"], 1)
                dve.wait_ge(sem["out_stored"], (g + 1) * 16)
                assert state["n"] == DVE_LINKS, state["n"]


def kernel(**inputs):
    import numpy as np
    import concourse.bacc as bacc
    from concourse.bass_utils import run_bass_kernel_spmd

    a = {n: np.asarray(v) for n, v in inputs.items()}
    f = np.float32

    weights = {
        "q1T": a["L0_xattn_Wq1"].T, "k1T": a["L0_xattn_Wk1"].T, "q2T": a["L0_xattn_Wq2"].T, "k2T": a["L0_xattn_Wk2"].T,
        "v1": a["L0_xattn_Wv1"], "v2": a["L0_xattn_Wv2"], "fc1": a["L0_xattn_fc1_w"], "fc2": a["L0_xattn_fc2_w"],
        "xqT": a["L1_xattn_Wq"].T, "xkT": a["L1_xattn_Wk"].T, "xvT": a["L1_xattn_Wv"].T, "xoT": a["L1_xattn_Wo"].T,
        "fq": a["L1_ffn_Wq"], "fk": a["L1_ffn_Wk"], "fv": a["L1_ffn_Wv"], "fo": a["L1_ffn_Wo"],
    }
    stacks = [np.tile(a["L1_xattn_Wq"].T[:, 32 * g:32 * g + 32], (1, 3)) for g in range(4)]
    wpack = np.concatenate([weights[n] for n in WNAMES] + stacks + [a["L1_ffn_gW"]], axis=1)
    cols = {"fc1": a["L0_xattn_fc1_b"], "xq": a["L1_xattn_bq"], "xk": a["L1_xattn_bk"], "xv": a["L1_xattn_bv"],
            "fq": a["L1_ffn_bq"], "fk": a["L1_ffn_bk"], "fv": a["L1_ffn_bv"]}
    pad = np.zeros(32, f)
    bq = [np.concatenate([np.tile(a["L1_xattn_bq"][32 * g:32 * g + 32], 3), pad]) for g in range(4)]
    cpack = np.stack([cols[n] for n in CNAMES] + list(a["L1_ffn_b1"].reshape(FT, D)) + bq, axis=1)
    rows = {"ln1g": a["L0_xattn_ln1_g"], "ln1b": a["L0_xattn_ln1_b"], "ln2g": a["L0_xattn_ln2_g"], "ln2b": a["L0_xattn_ln2_b"],
            "ln3g": a["L0_xattn_ln3_g"], "ln3b": a["L0_xattn_ln3_b"], "fc2b": a["L0_xattn_fc2_b"], "xbo": a["L1_xattn_bo"],
            "fbo": a["L1_ffn_bo"], "fln1g": a["L1_ffn_ln1_g"], "fln1b": a["L1_ffn_ln1_b"],
            "fln2g": a["L1_ffn_ln2_g"], "fln2b": a["L1_ffn_ln2_b"]}
    rpack = np.concatenate([rows[n] for n in RNAMES] + [a["L1_ffn_gb"], a["g_xattn"], a["g_ffn"]])
    kpack = np.zeros((D, KPACK), f)
    p = np.arange(D)
    kpack[:, K_ID:K_ID + D] = np.eye(D)
    kpack[:, K_M16:K_M16 + HEADS] = p[:, None] // HD == np.arange(HEADS)[None]
    kpack[:, K_M4:K_M4 + HG] = p[:, None] // HD % HG == np.arange(HG)[None]
    kpack[32:64, K_NEG1] = -1.0
    t = np.arange(T)
    kpack[:T, K_BASE:K_BASE + T] = np.where(t[None] <= t[:, None], -(t[None] + 0.5), -1e6)
    kpack[:REST, K_LAST:K_LAST + 32] = 1.0
    kpack[:, K_IOTA:K_IOTA + EXPERTS] = np.arange(EXPERTS)
    arrays = {
        "x": a["x"].transpose(1, 0, 2), "ctxn": a["ctx_1024"], "ctxt": a["ctx_1024"].transpose(0, 2, 1),
        "mask": a["mask_BxS2_bf1"].view(np.uint8), "wpack": wpack, "cpack": cpack, "rpack": rpack, "kpack": kpack,
        "w1": a["L1_ffn_W1"].transpose(1, 0, 2).reshape(D, FT * D),
        "w2": a["L1_ffn_W2"].reshape(FT, D, D).transpose(1, 0, 2).reshape(D, FT * D),
        "b2": a["L1_ffn_b2"],
        "wgu": np.concatenate([a["L0_ffn_w_gate"].T, a["L0_ffn_w_up"].T,
                               a["L0_ffn_w_down"].T.reshape(4, D, D).transpose(1, 0, 2).reshape(D, 4 * D)], axis=1),
    }
    nc = bacc.Bacc("TRN2", target_bir_lowering=False, num_devices=1)
    feeds, args = {}, []
    for name, value in arrays.items():
        value = np.ascontiguousarray(value)
        feeds[f"in_{name}"] = value
        args.append(nc.dram_tensor(f"in_{name}", value.shape, mybir.dt.from_np(value.dtype), kind="ExternalInput").ap())
    out = nc.dram_tensor("out_tokens", [T, BATCH, D], F32, kind="ExternalOutput").ap()
    build(nc, *args, out)
    r = run_bass_kernel_spmd(nc, [feeds], core_ids=[0])
    return np.ascontiguousarray(r.results[0]["out_tokens"].transpose(1, 0, 2))
```

```python
from contextlib import ExitStack

import concourse.bass as bass
from concourse import mybir

F32 = mybir.dt.float32
F32R = mybir.dt.float32r
BF16 = mybir.dt.bfloat16
U8 = mybir.dt.uint8
U32 = mybir.dt.uint32
ALU = mybir.AluOpType
ACT = mybir.ActivationFunctionType
AX = mybir.AxisListType

D = 128
T = 100
S = 1444
BATCH = 32
GROUP = 4
GROUPS = BATCH // GROUP
TG = GROUP * T
HEADS, HD = 16, 8
HG = 4
HQ = HEADS * T
KT = -(-S // D)
REST = S - (KT - 1) * D
CHUNK = 482
SPAD = 3 * CHUNK
PADK = KT * D
CHUNKS = [(c * CHUNK, min(CHUNK, S - c * CHUNK)) for c in range(3)]
QCH = -(-HQ // D)
PAIRED = 2 * 2 * T
INNER = 512
EXPERTS, FF = 8, 256
FT = EXPERTS * FF // D
EPS = 1e-5
DK_SCALE = float(HD) ** -0.5
ROUND = 12582912.0
PENALTY = float(2 ** 27)
CUT = 1e30
STACK = 99
JOBS = 3 + 3 + 3 * QCH + 1
KS_DMAS = 13
PAIR = 2 * GROUP
PAIRS = BATCH // PAIR
A_NORMS, A_TURNS = 6, 5
C_NORMS, C_TURNS = 3, 3
A_LOADS = (3, 3, 2)
GU = (1, 5)
DOWN = (7, 0)
HB = (0, 1, 4, 5)
A_LINKS, B_LINKS, C_LINKS = 158, 11, 64

WNAMES = ["q1T", "k1T", "q2T", "k2T", "v1", "v2", "fc1", "fc2", "xqT", "xkT", "xvT", "xo0", "xo1", "xo2", "xo3", "fq", "fk", "fv", "fo"]
WCOL = {n: i * D for i, n in enumerate(WNAMES)}
WSTACK = len(WNAMES) * D
WGATE = WSTACK + 4 * 96
WPACK = WGATE + EXPERTS
CNAMES = ["fc1", "xq", "xk", "xv0", "xv1", "fq", "fk", "fv"]
CCOL = {n: i for i, n in enumerate(CNAMES)}
CB1 = len(CNAMES)
CSTACK = CB1 + FT
CPACK = CSTACK + 4
RNAMES = ["ln1g", "ln1b", "ln2g", "ln2b", "ln3g", "ln3b", "fc2b", "xbo", "fbo", "fln1g", "fln1b", "fln2g", "fln2b"]
RROW = {n: i * D for i, n in enumerate(RNAMES)}
RGB = len(RNAMES) * D
RTANH = RGB + EXPERTS
RPACK = RTANH + 4
K_ID, K_M16, K_M4, K_NEG1, K_BASE, K_IOTA, K_SEL = 0, 128, 144, 148, 149, 249, 257
KPACK = K_SEL + 2 * D

SLOT_JOBS = JOBS + 1
RING = (4, 5, 7)
Q_PARTS = ((0, 136), (136, 132), (268, 132))
Q_JOBS = 3 + HG
PRO_JOBS = Q_JOBS + JOBS + 3
PLACES = 4 * KT
TURN_AT = 38


class Shared:
    pass

SIGNALS = """
a_chain a_cleared a_out_ready a_rstd_ready a_tokT_ready a_tok_ready a_tok_turned a_var_ready aqT_psum
aqT_ready aq_ready att_free att_ready attx_psum b2_psum b_chain b_cleared big_loaded c_chain c_cleared
c_rstd_ready c_tokT_ready c_tok_ready c_tok_turned c_var_ready c_x_loaded c_x_used consts_loaded down_psum
e1T_psum e1T_ready e1_ready e2_ready eg_ready f1_psum f1_ready f2_psum factors_ready feT_psum feT_ready
fe_ready fk_ready fo_psum fq_ready fqk_psum fs_psum fsub_ready fu_ready fv_psum fv_ready gate_psum gexp_ready
gsub_ready gu_psum gu_used h3t_stored ht_loaded kbd_ready kh_ready kl_ready len1_psum len1_ready m_turn_psum
max2_ready moe_h_psum moe_h_ready moe_y_psum moe_y_used mx_ready nm_ready ones_ready out_ready out_stored
pT_psum pT_ready pen_ready0 pen_stored pt_ready pv_done q_ready qbd_ready qexp_ready quotient_ready rT_ready
r_psum rd_ready ring_drained ring_filled row_ready s1_psum s2_psum s2m_psum setup_chain sm1_ready st_psum
v1_psum v1_ready v_cleared wT_psum wT_ready w_ready wo_psum wsum_psum wsum_ready x1_stored x_loaded x_used
z1_psum z2T_psum z2T_ready z2_psum
""".split()


def build(nc, x, ctxn, ctxt, mask, wpack, cpack, rpack, kpack, w1, w2, b2, wgu, out):
    with ExitStack() as ctx:
        def sb(name, shape, dt=F32):
            return ctx.enter_context(nc.sbuf_tensor(name, shape, dt))

        def dram(name, shape):
            return nc.dram_tensor(name, shape, F32, kind="Internal").ap()

        def places(name, count):
            return [ctx.enter_context(nc.semaphore(f"{name}{p}")) for p in range(count)]

        t = Shared()
        t.sem = {n: ctx.enter_context(nc.semaphore(n)) for n in SIGNALS}
        t.a_ct_loaded, t.a_cn_loaded = places("a_ct_loaded", 3), places("a_cn_loaded", 3)
        t.ct_loaded, t.ks_loaded = places("ct_loaded", 2), places("ks_loaded", 2)
        t.att_stored = places("att_stored", GROUP)
        t.qrow_loaded, t.mask_loaded = places("qrow_loaded", 2), places("mask_loaded", 2)
        t.psum = ctx.enter_context(nc.psum_tensor("psum", [D, 8, 512], F32))
        pen_dram = dram("pen_scratch", [BATCH, S])
        x1 = dram("x1_scratch", [T, BATCH, D])
        h3t = dram("h3t_scratch", [D, BATCH * T])
        att = dram("att_scratch", [D, BATCH * PAIRED])

        t.W = sb("W", [D, WPACK])
        t.C = sb("C", [D, CPACK])
        t.R = sb("R", [T, RPACK])
        t.K = sb("K", [D, KPACK])
        t.B2 = sb("B2", [EXPERTS, D])
        t.M12 = sb("M12", [D, 2 * D])
        t.wq_int = sb("wq_int", [D, 3 * INNER], BF16)
        t.wscale = sb("wscale", [D, 12])
        t.tanhs = sb("tanhs", [T, 4])
        t.ones = sb("ones", [D, D])
        t.cut_row = sb("cut_row", [1, D], BF16)
        t.xbq = sb("xbq", [D, 8])
        t.carrier = sb("carrier", [1, 1])
        t.ident = t.K[:, K_ID:K_ID + D]
        t.mask16 = t.K[:, K_M16:K_M16 + HEADS]
        t.mask4 = t.K[:, K_M4:K_M4 + HG]

        def w(name):
            return t.W[:, WCOL[name]:WCOL[name] + D]

        def col(name):
            return t.C[:, CCOL[name]:CCOL[name] + 1]

        def row(name):
            return t.R[:, RROW[name]:RROW[name] + D].unsqueeze(1).to_broadcast([T, GROUP, D])

        def bank(b, rows=D, cols=512, at=0):
            return t.psum[0:rows, b, at:at + cols]

        def tok_bank(b):
            return t.psum[0:T, b, :].rearrange("p (j d) -> p j d", j=GROUP)

        def ts_(j, n=T):
            return slice(j * n, (j + 1) * n)

        def linker(dve, chain):
            state = {"n": 0, "base": 0}

            def link(ins, plain=False):
                state["n"] += 1
                ins.then_inc(chain, 1)
                dve.wait_ge(chain, state["base"] + state["n"])
                if plain:
                    nc.vector.memset(t.carrier[:, :], 0.0)
            return link, state

        t.w, t.col, t.row, t.bank, t.tok_bank, t.ts_, t.linker = w, col, row, bank, tok_bank, ts_, linker
        setup(nc, t, mask, wpack, cpack, rpack, kpack, b2, wgu, pen_dram)
        stage_a(nc, t, x, ctxn, ctxt, x1, h3t)
        stage_b(nc, t, ctxt, mask, pen_dram, h3t, att)
        stage_c(nc, t, x1, att, w1, w2, out)


def setup(nc, t, mask, wpack, cpack, rpack, kpack, b2, wgu, pen_dram):
    with ExitStack() as ctx:
        sem, wscale = t.sem, t.wscale
        WRAW = ctx.enter_context(nc.sbuf_tensor("WRAW", [D, 3 * INNER], F32))
        WTMP = ctx.enter_context(nc.sbuf_tensor("WTMP", [D, 3 * INNER], F32))
        MB = ctx.enter_context(nc.sbuf_tensor("MB0", [BATCH, S], U8))
        PEN = ctx.enter_context(nc.sbuf_tensor("PEN", [BATCH, S], F32))
        PENR = ctx.enter_context(nc.sbuf_tensor("PENR", [BATCH, S], F32R))
        any_key = ctx.enter_context(nc.sbuf_tensor("any_key", [BATCH, 1], F32))
        block = ctx.enter_context(nc.Block())

        @block.sync
        def _(sp):
            for dst, src in ((WRAW, wgu), (MB, mask), (t.W, wpack), (t.C, cpack), (t.K, kpack),
                             (t.R, rpack.partition_broadcast(T)), (t.B2, b2)):
                sp.dma_start(dst[:, :], src).then_inc(sem["consts_loaded"], 16)
            sp.wait_ge(sem["pen_ready0"], 1)
            sp.dma_start(pen_dram, PENR[:, :].bitcast(F32)).then_inc(sem["pen_stored"], 16)
            sp.wait_ge(sem["pen_stored"], 16)

        @block.gpsimd
        def _(pool):
            nc.gpsimd.memset(t.cut_row[:, :], CUT)
            nc.gpsimd.memset(t.ones[:, :], 1.0).then_inc(sem["ones_ready"], 1)

        @block.scalar
        def _(act):
            act.wait_ge(sem["consts_loaded"], 112)
            nc.scalar.activation(t.tanhs[:, :], t.R[:, RTANH:RTANH + 4], ACT.Tanh)
            nc.scalar.mul(t.xbq[:, 0:1], t.col("xq"), DK_SCALE)
            nc.scalar.mul(t.xbq[:, 1:2], t.col("fq"), DK_SCALE)
            nc.scalar.mul(t.xbq[:, 2:6], t.C[:, CSTACK:CSTACK + 4], DK_SCALE)
            for n in range(2):
                act.wait_ge(sem["m_turn_psum"], n + 1)
                nc.scalar.copy(t.M12[:, t.ts_(n, D)], t.bank(n, D, D))

        @block.tensor
        def _(pe):
            mm = nc.tensor.matmul
            pe.wait_ge(sem["consts_loaded"], 112)
            for n, (a, b) in enumerate((("q1T", "k1T"), ("q2T", "k2T"))):
                mm(t.bank(n, D, D), t.w(a), t.w(b), start=True, stop=True).then_inc(sem["m_turn_psum"], 1)
            pe.wait_ge(sem["wsum_ready"], 1)
            pe.wait_ge(sem["ones_ready"], 1)
            mm(t.bank(2, D, 3), t.ones[:, :], wscale[:, 0:3], start=True, stop=True).then_inc(sem["wsum_psum"], 1)

        @block.vector
        def _(dve):
            v = nc.vector
            link, state = t.linker(dve, sem["setup_chain"])
            ts = v.tensor_scalar
            dve.wait_ge(sem["consts_loaded"], 112)
            wv = WRAW[:, :].rearrange("p (m c) -> p m c", m=3)
            v.tensor_reduce(wscale[:, 0:3], wv, AX.X, ALU.add, apply_absolute_value=True).then_inc(sem["wsum_ready"], 1)
            link(v.tensor_copy(PEN[:, :], MB[:, :]))
            link(v.tensor_reduce(any_key[:, :], PEN[:, :], AX.X, ALU.max))
            link(ts(any_key[:, :], any_key[:, :], PENALTY, None, ALU.mult))
            ts(PENR[:, :], PEN[:, :], -1.0, any_key[:, :], ALU.add, ALU.mult).then_inc(sem["pen_ready0"], 1)
            dve.wait_ge(sem["wsum_psum"], 1)
            link(ts(wscale[:, 3:6], t.bank(2, D, 3), 1.0 / (D * INNER), 1e-5, ALU.mult, ALU.max))
            link(v.reciprocal(wscale[:, 6:9], wscale[:, 3:6]))
            for m in range(3):
                last = ts(WTMP[:, m * INNER:(m + 1) * INNER], WRAW[:, m * INNER:(m + 1) * INNER],
                          wscale[:, 6 + m:7 + m], ROUND, ALU.mult, ALU.add)
            link(last)
            link(ts(WTMP[:, :], WTMP[:, :], -ROUND, 1.0, ALU.add, ALU.min))
            ts(t.wq_int[:, :], WTMP[:, :], -1.0, None, ALU.max)


def stage_a(nc, t, x, ctxn, ctxt, x1, h3t):
    with ExitStack() as ctx:
        def sb(name, shape, dt=F32):
            return ctx.enter_context(nc.sbuf_tensor("a_" + name, shape, dt))

        sem, psum, K, wscale, tanhs, ident = t.sem, t.psum, t.K, t.wscale, t.tanhs, t.ident
        w, col, row, bank, tok_bank = t.w, t.col, t.row, t.bank, t.tok_bank
        XIN = sb("XIN", [T, 2, GROUP, D])
        X = sb("X", [T, 2, GROUP, D])
        H = sb("H", [T, 2, GROUP, D])
        U = sb("U", [T, 2, GROUP, D])
        Y = sb("Y", [T, 2, GROUP, D])
        VS = sb("VS", [T, 2, GROUP, D])
        HT = sb("HT", [D, 2, TG])
        HOUT = sb("HOUT", [D, 2, TG])
        RT = sb("RT", [D, 2, TG])
        AT = sb("AT", [D, 2, TG])
        HQT = sb("HQT", [D, 2, TG], BF16)
        E1 = sb("E1", [T, 2, GROUP, T])
        E1T = sb("E1T", [T, 2, TG])
        CT = sb("CT", [D, 3, SPAD])
        CN = sb("CN", [D, 3, KT, D])
        PJ = sb("PJ", [T, 2, SPAD])
        PTA = sb("PTA", [D, 2, KT, T])
        EG = sb("EG", [T, 2, INNER])
        AQ = sb("AQ", [T, 2, INNER])
        AQT = sb("AQT", [D, 2, TG], BF16)
        stats_ = sb("stats", [T, 2, GROUP, 6])
        mv = sb("mv", [T, 2, GROUP, 2])
        ve = sb("ve", [T, 2, GROUP])
        rs = sb("rs", [T, 2, GROUP])
        sm = sb("sm", [T, 2, 16, GROUP])
        len1 = sb("len1", [1, 2, GROUP])
        len2 = sb("len2", [1, 1])
        nz = sb("nz", [1, SPAD])
        prow = sb("prow", [1, 2, SPAD], BF16)
        key_row = sb("key_row", [1, SPAD])
        half = sb("half", [T, GROUP])

        block = ctx.enter_context(nc.Block())

        @block.sync
        def _(sp):
            def load_x(i):
                sp.dma_start(XIN[:, :, :, :].rearrange("p h j d -> p (h j) d"),
                             x[:, bass.ds(i * PAIR, PAIR), :]).then_inc(sem["x_loaded"], 16)

            def load_ctx(i, m):
                n = i * PAIR + m
                src = ctxn[n]
                sp.dma_start(CT[:, m % 3, 0:S], ctxt[n]).then_inc(t.a_ct_loaded[m % 3], 16)
                sp.dma_start(CN[:, m % 3, 0:KT - 1, :],
                             src[0:(KT - 1) * D, :].rearrange("(k p) d -> p k d", p=D)).then_inc(t.a_cn_loaded[m % 3], 16)
                sp.dma_start(CN[0:REST, m % 3, KT - 1, :], src[(KT - 1) * D:S, :]).then_inc(t.a_cn_loaded[m % 3], 16)

            def pair(i, more):
                for m in range(3, PAIR):
                    sp.wait_ge(sem["z2T_psum"], i * PAIR + m - 2)
                    load_ctx(i, m)
                if more:
                    sp.wait_ge(sem["x_used"], 2 * i + 2)
                    load_x(i + 1)
                    sp.wait_ge(sem["z2T_psum"], (i + 1) * PAIR)
                    for m in range(3):
                        load_ctx(i + 1, m)
                for h in range(2):
                    sp.wait_ge(sem["a_out_ready"], 2 * i + h + 1)
                    sp.dma_start(x1[:, bass.ds((2 * i + h) * GROUP, GROUP), :], X[:, h, :, :]).then_inc(sem["x1_stored"], 16)
                for h in range(2):
                    sp.wait_ge(sem["a_tokT_ready"], (i * A_TURNS + 4) * 2 + h + 1)
                    sp.dma_start(h3t[:, bass.ds((2 * i + h) * TG, TG)], HOUT[:, h, :]).then_inc(sem["h3t_stored"], 16)

            load_x(0)
            for m in range(3):
                load_ctx(0, m)
            with sp.Fori(0, PAIRS - 1) as i:
                pair(i, True)
            pair(PAIRS - 1, False)
            sp.wait_ge(sem["x1_stored"], 32 * PAIRS + 1)
            sp.wait_ge(sem["h3t_stored"], 32 * PAIRS + 1)

        @block.gpsimd
        def _(pool):
            nc.gpsimd.memset(half[:, :], -0.5)
            nc.gpsimd.memset(CT[:, :, S:SPAD], 0.0)
            nc.gpsimd.iota(key_row[:, :], [[-1, SPAD]], base=0, channel_multiplier=0,
                           allow_small_or_imprecise_dtypes=True).then_inc(sem["a_cleared"], 1)
            pool.wait_ge(sem["a_cleared"], 1)
            with pool.Fori(0, PAIRS) as i:
                for k in range(A_NORMS):
                    for h in range(2):
                        pool.wait_ge(sem["a_var_ready"], (i * A_NORMS + k) * 2 + h + 1)
                        nc.gpsimd.tensor_tensor(rs[:, h, :], ve[:, h, :], half[:, :], ALU.pow).then_inc(sem["a_rstd_ready"], 1)

        @block.scalar
        def _(act):
            with act.Fori(0, PAIRS) as i:
                def turned(k, dst, b=0, **kw):
                    for h in range(2):
                        act.wait_ge(sem["a_tok_turned"], (i * A_TURNS + k) * 2 + h + 1)
                        nc.scalar.activation(dst[:, h, :], bank(4 * h + b, D, TG), ACT.Copy, **kw).then_inc(sem["a_tokT_ready"], 1)

                turned(0, HT)
                for h in range(2):
                    act.wait_ge(sem["r_psum"], 4 * i + h + 1)
                    nc.scalar.copy(RT[:, h, :], bank(4 * h + 1, D, TG)).then_inc(sem["rT_ready"], 1)
                for h in range(2):
                    act.wait_ge(sem["v1_psum"], 2 * i + h + 1)
                    nc.scalar.copy(VS[:, h, :, :], tok_bank(4 * h + 2)).then_inc(sem["v1_ready"], 1)
                for h in range(2):
                    act.wait_ge(sem["sm1_ready"], 2 * i + h + 1)
                    for j in range(GROUP):
                        e = nc.scalar.activation(E1[:, h, j, :], E1[:, h, j, :], ACT.Exp, scale=DK_SCALE,
                                                 bias=sm[:, h, 1, j:j + 1], accum_out=sm[:, h, 2, j:j + 1])
                    e.then_inc(sem["e1_ready"], 1)
                for h in range(2):
                    act.wait_ge(sem["e1T_psum"], 2 * i + h + 1)
                    nc.scalar.copy(E1T[:, h, :], bank(4 * h, T, TG)).then_inc(sem["e1T_ready"], 1)
                turned(1, HT)
                for h in range(2):
                    act.wait_ge(sem["r_psum"], 4 * i + 2 + h + 1)
                    nc.scalar.copy(RT[:, h, :], bank(4 * h + 1, D, TG)).then_inc(sem["rT_ready"], 1)

                def probabilities(m):
                    h, j = divmod(m, GROUP)
                    act.wait_ge(sem["max2_ready"], i * PAIR + m + 1)
                    if m >= 2:
                        act.wait_ge(sem["pT_psum"], (i * PAIR + m - 1) * 3)
                    nc.scalar.activation(PJ[:, m % 2, :].rearrange("p (c k) -> p c k", c=3),
                                         psum[0:T, 3 * (m % 2):3 * (m % 2) + 3, 0:CHUNK], ACT.Exp,
                                         scale=DK_SCALE, bias=sm[:, h, 4, j:j + 1],
                                         accum_out=sm[:, h, 5, j:j + 1]).then_inc(sem["e2_ready"], 1)

                probabilities(0)
                for m in range(PAIR):
                    n = i * PAIR + m
                    for r in range(3):
                        act.wait_ge(sem["pT_psum"], n * 3 + r + 1)
                        if r == 0 and m >= 2:
                            act.wait_ge(sem["z2T_psum"], n - 1)
                        if r < 2:
                            nc.scalar.copy(PTA[:, m % 2, 4 * r:4 * r + 4, :],
                                           bank(6 + r, D, TG).rearrange("p (k t) -> p k t", k=4)).then_inc(sem["pT_ready"], 1)
                        else:
                            nc.scalar.copy(PTA[:, m % 2, 8:11, :], bank(6, D, 3 * T).rearrange("p (k t) -> p k t", k=3))
                            nc.scalar.copy(PTA[0:REST, m % 2, 11, :], bank(6, REST, T, 3 * T)).then_inc(sem["pT_ready"], 1)
                    if m + 1 < PAIR:
                        probabilities(m + 1)
                    act.wait_ge(sem["z2T_psum"], n + 1)
                    nc.scalar.copy(AT[:, m // GROUP, t.ts_(m % GROUP)], bank(7, D, T, TG)).then_inc(sem["z2T_ready"], 1)
                turned(2, HT)
                for h in range(2):
                    act.wait_ge(sem["f1_psum"], 2 * i + h + 1)
                    nc.scalar.activation(RT[:, h, :], bank(4 * h + 2, D, TG), ACT.Relu, bias=col("fc1")).then_inc(sem["f1_ready"], 1)
                for h in range(2):
                    act.wait_ge(sem["a_tok_turned"], (i * A_TURNS + 3) * 2 + h + 1)
                    nc.scalar.activation(HQT[:, h, :], bank(4 * h, D, TG), ACT.Copy, bias=-ROUND).then_inc(sem["a_tokT_ready"], 1)

                def gate(m):
                    h, j = divmod(m, GROUP)
                    n = i * PAIR + m
                    act.wait_ge(sem["gu_psum"], n + 1)
                    act.wait_ge(sem["factors_ready"], 2 * i + h + 1)
                    if m >= 2:
                        act.wait_ge(sem["aq_ready"], n - 1)
                    nc.scalar.activation(EG[:, m % 2, :], bank(GU[m % 2], T, INNER), ACT.Tanh,
                                         scale=sm[:, h, 9, j:j + 1]).then_inc(sem["eg_ready"], 1)

                gate(0)
                for m in range(PAIR):
                    if m + 1 < PAIR:
                        gate(m + 1)
                    act.wait_ge(sem["aqT_psum"], i * PAIR + m + 1)
                    if m >= 2:
                        act.wait_ge(sem["down_psum"], i * PAIR + m - 1)
                    nc.scalar.activation(AQT[:, m % 2, :], bank(3 + m % 2, D, TG), ACT.Copy, bias=-ROUND)\
                        .then_inc(sem["aqT_ready"], 1)
                for h in range(2):
                    act.wait_ge(sem["a_tok_turned"], (i * A_TURNS + 4) * 2 + h + 1)
                    act.wait_ge(sem["h3t_stored"], 32 * i + 1)
                    nc.scalar.copy(HOUT[:, h, :], bank(4 * h + 1, D, TG)).then_inc(sem["a_tokT_ready"], 1)

        @block.tensor
        def _(pe):
            mm = nc.tensor.matmul
            with pe.Fori(0, PAIRS) as i:
                def turn(k, src, b=0):
                    for h in range(2):
                        pe.wait_ge(sem["a_tok_ready"], (i * A_TURNS + k) * 2 + h + 1)
                        for j in range(GROUP):
                            m = nc.tensor.transpose(bank(4 * h + b, D, T, j * T), src[:, h, j, :], ident[0:T, 0:T])
                        m.then_inc(sem["a_tok_turned"], 1)

                def wait_turned(k, h):
                    pe.wait_ge(sem["a_tokT_ready"], (i * A_TURNS + k) * 2 + h + 1)

                def per_seq(b, lhsT, rhs, sig):
                    for j in range(GROUP):
                        m = mm(bank(b, T, D, j * D), lhsT[:, t.ts_(j)], rhs, start=True, stop=True)
                    m.then_inc(sem[sig], 1)

                turn(0, H)
                for h in range(2):
                    wait_turned(0, h)
                    mm(bank(4 * h + 1, D, TG), t.M12[:, 0:D], HT[:, h, :], start=True, stop=True).then_inc(sem["r_psum"], 1)
                    per_seq(4 * h + 2, HT[:, h, :], w("v1"), "v1_psum")
                for h in range(2):
                    pe.wait_ge(sem["rT_ready"], 4 * i + h + 1)
                    for j in range(GROUP):
                        m = mm(bank(4 * h + 3, T, T, j * T), RT[:, h, t.ts_(j)], HT[:, h, t.ts_(j)], start=True, stop=True)
                    m.then_inc(sem["s1_psum"], 1)
                for h in range(2):
                    pe.wait_ge(sem["len1_ready"], 2 * i + h + 1)
                    mm(bank(4 * h + 1, T, GROUP), t.ones[0:1, 0:T], len1[:, h, :], start=True, stop=True).then_inc(sem["len1_psum"], 1)
                for h in range(2):
                    pe.wait_ge(sem["e1_ready"], 2 * i + h + 1)
                    for j in range(GROUP):
                        m = nc.tensor.transpose(bank(4 * h, T, T, j * T), E1[:, h, j, :], ident[0:T, 0:T])
                    m.then_inc(sem["e1T_psum"], 1)
                for h in range(2):
                    pe.wait_ge(sem["e1T_ready"], 2 * i + h + 1)
                    pe.wait_ge(sem["v1_ready"], 2 * i + h + 1)
                    for j in range(GROUP):
                        m = mm(bank(4 * h + 2, T, D, j * D), E1T[:, h, t.ts_(j)], VS[:, h, j, :], start=True, stop=True)
                    m.then_inc(sem["z1_psum"], 1)
                turn(1, Y)
                for h in range(2):
                    wait_turned(1, h)
                    mm(bank(4 * h + 1, D, TG), t.M12[:, D:2 * D], HT[:, h, :], start=True, stop=True).then_inc(sem["r_psum"], 1)

                def scores(m):
                    h, j = divmod(m, GROUP)
                    if m < 2:
                        pe.wait_ge(sem["rT_ready"], 4 * i + 2 + m + 1)
                    pe.wait_ge(t.a_ct_loaded[m % 3], (A_LOADS[m % 3] * i + m // 3 + 1) * 16)
                    if m >= 2:
                        pe.wait_ge(sem["e2_ready"], i * PAIR + m - 1)
                    for c in range(3):
                        x_ = mm(bank(3 * (m % 2) + c, T, CHUNK), RT[:, h, t.ts_(j)],
                                CT[:, m % 3, c * CHUNK:(c + 1) * CHUNK], start=True, stop=True)
                    x_.then_inc(sem["s2_psum"], 1)

                def cut(m):
                    pe.wait_ge(sem["row_ready"], i * PAIR + m + 1)
                    for c in range(3):
                        x_ = mm(bank(3 * (m % 2) + c, T, CHUNK), t.cut_row[:, 0:T],
                                prow[:, m % 2, c * CHUNK:(c + 1) * CHUNK], start=False, stop=True, skip_group_check=True)
                    x_.then_inc(sem["s2m_psum"], 1)

                scores(0)
                cut(0)
                for m in range(PAIR):
                    n = i * PAIR + m
                    if m + 1 < PAIR:
                        scores(m + 1)
                    pe.wait_ge(sem["e2_ready"], n + 1)
                    for r in range(3):
                        if r == 1 and m:
                            pe.wait_ge(sem["z2T_ready"], n)
                        if r == 2:
                            pe.wait_ge(sem["pT_ready"], n * 3 + 1)
                        for k in range(4 * r, 4 * r + 4):
                            rows = D if k < KT - 1 else REST
                            x_ = nc.tensor.transpose(bank(6 + r % 2, rows, T, (k % 4) * T), PJ[:, m % 2, k * D:k * D + rows],
                                                     ident[0:T, 0:T])
                        x_.then_inc(sem["pT_psum"], 1)
                    if m + 1 < PAIR:
                        cut(m + 1)
                    pe.wait_ge(t.a_cn_loaded[m % 3], (A_LOADS[m % 3] * i + m // 3 + 1) * 32)
                    pe.wait_ge(sem["pT_ready"], n * 3 + 3)
                    for k in range(KT):
                        rows = D if k < KT - 1 else REST
                        x_ = mm(bank(7, D, T, TG), CN[0:rows, m % 3, k, :], PTA[0:rows, m % 2, k, :],
                                start=(k == 0), stop=(k == KT - 1))
                    x_.then_inc(sem["z2T_psum"], 1)
                for h in range(2):
                    pe.wait_ge(sem["z2T_ready"], i * PAIR + (h + 1) * GROUP)
                    per_seq(4 * h, AT[:, h, :], w("v2"), "z2_psum")
                turn(2, Y)
                for h in range(2):
                    wait_turned(2, h)
                    mm(bank(4 * h + 2, D, TG), w("fc1"), HT[:, h, :], start=True, stop=True).then_inc(sem["f1_psum"], 1)
                for h in range(2):
                    pe.wait_ge(sem["f1_ready"], 2 * i + h + 1)
                    per_seq(4 * h + 3, RT[:, h, :], w("fc2"), "f2_psum")
                turn(3, U)

                def gate_up(m):
                    h, j = divmod(m, GROUP)
                    if m >= 2:
                        pe.wait_ge(sem["gu_used"], i * PAIR + m - 1)
                    b = GU[m % 2]
                    mm(bank(b, T), HQT[:, h, t.ts_(j)], t.wq_int[:, 0:INNER], start=True, stop=True)
                    mm(bank(b + 1, T), HQT[:, h, t.ts_(j)], t.wq_int[:, INNER:2 * INNER], start=True, stop=True)\
                        .then_inc(sem["gu_psum"], 1)

                wait_turned(3, 0)
                gate_up(0)
                gate_up(1)
                for m in range(PAIR):
                    n = i * PAIR + m
                    pe.wait_ge(sem["aq_ready"], n + 1)
                    if m == 1:
                        wait_turned(3, 1)
                    elif m >= 2:
                        pe.wait_ge(sem["aqT_ready"], n - 1)
                    for c in range(4):
                        x_ = nc.tensor.transpose(bank(3 + m % 2, D, T, c * T), AQ[:, m % 2, c * D:(c + 1) * D], ident[0:T, 0:T])
                    x_.then_inc(sem["aqT_psum"], 1)
                    if m + 2 < PAIR:
                        gate_up(m + 2)
                    pe.wait_ge(sem["aqT_ready"], n + 1)
                    for c in range(4):
                        x_ = mm(bank(DOWN[m // GROUP], T, D, (m % GROUP) * D), AQT[:, m % 2, t.ts_(c)],
                                t.wq_int[:, 2 * INNER + c * D:2 * INNER + (c + 1) * D], start=(c == 0), stop=(c == 3))
                    x_.then_inc(sem["down_psum"], 1)
                turn(4, U, 1)
                wait_turned(4, 0)
                wait_turned(4, 1)

        @block.vector
        def _(dve):
            v = nc.vector
            link, state = t.linker(dve, sem["a_chain"])
            ts = v.tensor_scalar
            dve.wait_ge(sem["a_cleared"], 1)
            v.memset(t.carrier[:, :], 0.0).then_inc(sem["x1_stored"], 1)
            dve.wait_ge(sem["x1_stored"], 1)
            v.memset(t.carrier[:, :], 0.0).then_inc(sem["h3t_stored"], 1)
            dve.wait_ge(sem["h3t_stored"], 1)
            with dve.Fori(0, PAIRS) as i:
                state["n"] = 0
                state["base"] = i * A_LINKS

                def tok_done(ins, k, h):
                    ins.then_inc(sem["a_tok_ready"], 1)
                    dve.wait_ge(sem["a_tok_ready"], (i * A_TURNS + k) * 2 + h + 1)

                def moments(h, src):
                    for j in range(GROUP):
                        last = v.bn_stats(stats_[:, h, j, :], src[:, h, j, :])
                    link(last, plain=True)
                    for j in range(GROUP):
                        last = v.bn_aggr(mv[:, h, j, :], stats_[:, h, j, :])
                    link(last)
                    ts(ve[:, h, :], mv[:, h, :, 1], EPS, None, ALU.add).then_inc(sem["a_var_ready"], 1)

                def normed(k, h, src, dst, gain=None):
                    dve.wait_ge(sem["a_rstd_ready"], (i * A_NORMS + k) * 2 + h + 1)
                    for j in range(GROUP):
                        last = ts(dst[:, h, j, :], src[:, h, j, :], mv[:, h, j, 0:1], rs[:, h, j:j + 1],
                                  ALU.subtract, ALU.mult)
                    if gain is None:
                        return last
                    link(last)
                    link(v.tensor_tensor(dst[:, h, :, :], dst[:, h, :, :], row(gain + "g"), ALU.mult))
                    return v.tensor_tensor(dst[:, h, :, :], dst[:, h, :, :], row(gain + "b"), ALU.add)

                def quantise(src, dst, amax, scale):
                    n = amax.shape[1]
                    link(v.tensor_reduce(amax, src, AX.X, ALU.max, apply_absolute_value=True))
                    link(ts(amax, amax, 1e-5, None, ALU.max))
                    link(v.reciprocal(scale, amax))
                    link(ts(scale, scale, 127.0, None, ALU.mult))
                    for j in range(n):
                        last = ts(dst[:, j, :] if n > 1 else dst, src[:, j, :] if n > 1 else src, scale[:, j:j + 1], ROUND,
                                  ALU.mult, ALU.add)
                    link(last)
                    return ts(dst, dst, ROUND + 127.0, ROUND - 128.0, ALU.min, ALU.max)

                dve.wait_ge(sem["x_loaded"], (i + 1) * 16)
                for h in range(2):
                    moments(h, XIN)
                for h in range(2):
                    tok_done(normed(0, h, XIN, H), 0, h)
                for h in range(2):
                    dve.wait_ge(sem["s1_psum"], 2 * i + h + 1)
                    s1 = psum[0:T, 4 * h + 3, 0:TG].rearrange("p (j k) -> p j k", j=GROUP)
                    link(ts(E1[0:1, h, :, :], s1[0:1, :, :], 0.0, None, ALU.not_equal))
                    v.tensor_reduce(len1[:, h, :], E1[0:1, h, :, :], AX.X, ALU.add).then_inc(sem["len1_ready"], 1)
                for h in range(2):
                    s1 = psum[0:T, 4 * h + 3, 0:TG].rearrange("p (j k) -> p j k", j=GROUP)
                    s = sm[:, h, :, :]
                    E = E1[:, h, :, :]
                    dve.wait_ge(sem["len1_psum"], 2 * i + h + 1)
                    link(v.tensor_copy(s[:, 3, :], bank(4 * h + 1, T, GROUP)))
                    base = K[0:T, K_BASE:K_BASE + T].unsqueeze(1).to_broadcast([T, GROUP, T])
                    link(v.tensor_tensor(E, base, s[:, 3, :].unsqueeze(2).to_broadcast([T, GROUP, T]), ALU.add))
                    link(ts(E, E, 0.0, CUT, ALU.min, ALU.mult))
                    link(v.tensor_tensor(E, s1, E, ALU.add))
                    link(v.tensor_reduce(s[:, 0, :], E, AX.X, ALU.max))
                    ts(s[:, 1, :], s[:, 0, :], -DK_SCALE, None, ALU.mult).then_inc(sem["sm1_ready"], 1)
                for h in range(2):
                    dve.wait_ge(sem["e1_ready"], 2 * i + h + 1)
                    link(v.reciprocal(sm[:, h, 2, :], sm[:, h, 2, :]))
                for h in range(2):
                    dve.wait_ge(sem["z1_psum"], 2 * i + h + 1)
                    for j in range(GROUP):
                        last = v.scalar_tensor_tensor(out=U[:, h, j, :], in0=tok_bank(4 * h + 2)[:, j, :],
                                                      scalar=sm[:, h, 2, j:j + 1], in1=H[:, h, j, :],
                                                      op0=ALU.mult, op1=ALU.add)
                    link(last)
                    moments(h, U)
                for h in range(2):
                    tok_done(normed(1, h, U, Y, "ln1"), 1, h)
                for m in range(PAIR):
                    h, j = divmod(m, GROUP)
                    n = i * PAIR + m
                    sc = psum[0:T, 3 * (m % 2):3 * (m % 2) + 3, 0:CHUNK]
                    dve.wait_ge(sem["s2_psum"], n + 1)
                    link(ts(nz[:, :].rearrange("p (c k) -> p c k", c=3), sc[0:1, :, :], 0.0, None, ALU.not_equal, ALU.add,
                            accum_out=len2[:, :]))
                    link(ts(nz[:, :], key_row[:, :], len2[:, :], -0.5, ALU.add, ALU.add))
                    if m >= 2:
                        dve.wait_ge(sem["s2m_psum"], n - 1)
                    ts(prow[:, m % 2, :], nz[:, :], 0.0, None, ALU.min).then_inc(sem["row_ready"], 1)
                    dve.wait_ge(sem["row_ready"], n + 1)
                    dve.wait_ge(sem["s2m_psum"], n + 1)
                    link(v.tensor_reduce(sm[:, h, 6, j:j + 1], sc, AX.XY, ALU.max))
                    ts(sm[:, h, 4, j:j + 1], sm[:, h, 6, j:j + 1], -DK_SCALE, None, ALU.mult).then_inc(sem["max2_ready"], 1)
                for h in range(2):
                    dve.wait_ge(sem["e2_ready"], i * PAIR + (h + 1) * GROUP)
                    link(v.reciprocal(sm[:, h, 5, :], sm[:, h, 5, :]))
                for h in range(2):
                    dve.wait_ge(sem["z2_psum"], 2 * i + h + 1)
                    for j in range(GROUP):
                        last = v.scalar_tensor_tensor(out=U[:, h, j, :], in0=tok_bank(4 * h)[:, j, :],
                                                      scalar=sm[:, h, 5, j:j + 1], in1=Y[:, h, j, :],
                                                      op0=ALU.mult, op1=ALU.add)
                    link(last)
                    moments(h, U)
                for h in range(2):
                    tok_done(normed(2, h, U, Y, "ln2"), 2, h)
                for h in range(2):
                    dve.wait_ge(sem["f2_psum"], 2 * i + h + 1)
                    link(v.tensor_tensor(U[:, h, :, :], tok_bank(4 * h + 3), row("fc2b"), ALU.add))
                    link(v.tensor_tensor(U[:, h, :, :], U[:, h, :, :], Y[:, h, :, :], ALU.add))
                    moments(h, U)
                dve.wait_ge(sem["x1_stored"], 32 * i + 1)
                for h in range(2):
                    link(normed(3, h, U, Y, "ln3"))
                    v.scalar_tensor_tensor(out=X[:, h, :, :], in0=Y[:, h, :, :], scalar=tanhs[:, 0:1], in1=XIN[:, h, :, :],
                                           op0=ALU.mult, op1=ALU.add).then_inc(sem["x_used"], 1)
                    dve.wait_ge(sem["x_used"], 2 * i + h + 1)
                    moments(h, X)
                for h in range(2):
                    s = sm[:, h, :, :]
                    link(normed(4, h, X, H))
                    tok_done(quantise(H[:, h, :, :], U[:, h, :, :], s[:, 7, :], s[:, 8, :]), 3, h)
                    ts(s[:, 9, :], s[:, 7, :], wscale[0:T, 3:4], 0.5 / 127.0, ALU.mult, ALU.mult)
                    link(ts(s[:, 11, :], s[:, 7, :], wscale[0:T, 4:5], 1.0 / 127.0, ALU.mult, ALU.mult))
                    v.tensor_tensor(s[:, 10, :], s[:, 9, :], s[:, 11, :], ALU.mult)
                    link(ts(s[:, 12, 0:1], wscale[0:T, 5:6], tanhs[:, 2:3], None, ALU.mult))
                    ts(s[:, 12, 0:1], s[:, 12, 0:1], 1.0 / 127.0, None, ALU.mult).then_inc(sem["factors_ready"], 1)
                    dve.wait_ge(sem["factors_ready"], 2 * i + h + 1)
                for m in range(PAIR):
                    h, j = divmod(m, GROUP)
                    n = i * PAIR + m
                    s = sm[:, h, :, :]
                    b = GU[m % 2]
                    E = EG[:, m % 2, :]
                    dve.wait_ge(sem["eg_ready"], n + 1)
                    link(v.scalar_tensor_tensor(out=E, in0=E, scalar=1.0, in1=bank(b, T), op0=ALU.add, op1=ALU.mult))
                    v.scalar_tensor_tensor(out=E, in0=bank(b + 1, T), scalar=s[:, 10, j:j + 1], in1=E,
                                           op0=ALU.mult, op1=ALU.mult).then_inc(sem["gu_used"], 1)
                    dve.wait_ge(sem["gu_used"], n + 1)
                    if m >= 2:
                        dve.wait_ge(sem["aqT_psum"], n - 1)
                    quantise(E, AQ[:, m % 2, :], s[:, 13, j:j + 1], s[:, 14, j:j + 1]).then_inc(sem["aq_ready"], 1)
                    link(ts(s[:, 15, j:j + 1], s[:, 13, j:j + 1], s[:, 12, 0:1], None, ALU.mult))
                for h in range(2):
                    dve.wait_ge(sem["down_psum"], i * PAIR + (h + 1) * GROUP)
                    for j in range(GROUP):
                        last = v.scalar_tensor_tensor(out=X[:, h, j, :], in0=tok_bank(DOWN[h])[:, j, :],
                                                      scalar=sm[:, h, 15, j:j + 1], in1=X[:, h, j, :],
                                                      op0=ALU.mult, op1=ALU.add)
                    last.then_inc(sem["a_out_ready"], 1)
                    dve.wait_ge(sem["a_out_ready"], 2 * i + h + 1)
                    moments(h, X)
                for h in range(2):
                    tok_done(normed(5, h, X, U), 4, h)
                assert state["n"] == A_LINKS, state["n"]


def ring_jobs(g, j, last):
    result = [(g, j + 1, "result", 0)]
    if last and j + 1 == GROUP:
        return result
    score = [(g, j + 1, "score", r) for r in range(3 * QCH)]
    value = [(g, j + 1, "value", r) for r in range(3)]
    jobs = score[0:4] + result + score[4:8] + value[0:1] + score[8:12] + value[1:2] + score[12:16] + value[2:3] + score[16:]
    jobs.append((g, j + 1, "turn", 0))
    if j == GROUP - 2 and not last:
        jobs += [(g + 1, 0, "query", r) for r in range(Q_JOBS)]
    if not last or j + 2 < GROUP:
        jobs += [(g, j + 2, "key", r) for r in range(3)]
    return jobs


def ring_place(jobs, i):
    early = sum(kind in ("score", "value", "turn", "result") for _, _, kind, _ in jobs)
    if i < early:
        return i * TURN_AT // early
    return TURN_AT + (i - early) * (PLACES - TURN_AT) // (len(jobs) - early)


def first_ring_jobs():
    return [(0, 0, "query", r) for r in range(Q_JOBS)] + [(0, 0, "key", r) for r in range(3)] \
        + [job for job in ring_jobs(0, -1, False) if job[2] != "result"]


def stage_b(nc, t, ctxt, mask, pen_dram, h3t, att):
    with ExitStack() as ctx:
        def sb(name, shape, dt=F32):
            return ctx.enter_context(nc.sbuf_tensor("b_" + name, shape, dt))

        sem, psum, K, W, xbq = t.sem, t.psum, t.K, t.W, t.xbq
        w, col, bank, ts_ = t.w, t.col, t.bank, t.ts_
        HT = sb("HT", [D, TG])
        QT = sb("QT", [D, TG])
        QF = sb("QF", [96, TG])
        QH = sb("QH", [96, TG], F32R)
        QR = sb("QR", [96, HG, TG], F32R)
        CT = sb("CT", [D, 2, SPAD])
        V = sb("V", [D, 2, KT, 8, 32])
        MB = sb("MB", [D, 2, S], U8)
        KF = sb("KF", [D, SPAD])
        KH = sb("KH", [D, S], F32R)
        KL = sb("KL", [D, S], F32R)
        KS = sb("KS", [D, 2, HG, PADK], F32R)
        QBD = sb("QBD", [D, QCH * D], F32R)
        QS = sb("QS", [D, 2, QCH * D], F32R)
        PT = sb("PT", [D, 2, HG, TG])
        OD = sb("OD", [D, PAIRED])
        RD = sb("RD", [D, PAIRED // 2])
        AO = sb("AO", [D, GROUP, PAIRED])
        part_max = sb("part_max", [D, QCH, 3])
        mx = sb("mx", [D, 16])
        NMH = sb("NMH", [QCH, D], F32R)
        NML = sb("NML", [QCH, D], F32R)

        def wait(engine, semaphore, value):
            if not (isinstance(value, int) and value <= 0):
                engine.wait_ge(semaphore, value)

        def bank_number(g, j, i, last):
            at = PRO_JOBS + sum(len(ring_jobs(g, s, last)) for s in range(j)) + i
            return g * (GROUP * SLOT_JOBS + Q_JOBS) + at, at % len(RING)

        END = sum(len(ring_jobs(g, j, g == GROUPS - 1)) for g in range(GROUPS) for j in range(GROUP)) + PRO_JOBS

        block = ctx.enter_context(nc.Block())

        @block.sync
        def _(sp):
            def load_ct(g, j):
                sp.dma_start(CT[:, j % 2, 0:S], ctxt[g * GROUP + j]).then_inc(t.ct_loaded[j % 2], 16)

            def load_mask(g, j):
                sp.dma_start(MB[:, j % 2, :], mask[g * GROUP + j].partition_broadcast(D)).then_inc(t.mask_loaded[j % 2], 16)

            def load_ht(g):
                sp.dma_start(HT[:, :], h3t[:, bass.ds(g * TG, TG)]).then_inc(sem["ht_loaded"], 16)

            def stack_keys(g, j):
                n = g * GROUP + j
                for hg in range(HG):
                    for r, part in enumerate((KH, KH, KL)):
                        sp.dma_start(KS[32 * r:32 * r + 32, j % 2, hg, 0:S].bitcast(F32),
                                     part[32 * hg:32 * hg + 32, 0:S].bitcast(F32)).then_inc(t.ks_loaded[j % 2], 16)
                sp.dma_start(KS[98:99, j % 2, :, 0:S].bitcast(F32),
                             pen_dram[bass.ds(n, 1), :].unsqueeze(1).to_broadcast([1, HG, S]))\
                  .then_inc(t.ks_loaded[j % 2], 16)

            def stack_maxima(g, j):
                sp.wait_ge(sem["nm_ready"], g * GROUP + (j + 1))
                for r, part in enumerate((NMH, NML)):
                    sp.dma_start(QS[96 + r:97 + r, j % 2, :].bitcast(F32), part[:, :].bitcast(F32)).then_inc(t.qrow_loaded[j % 2], 16)

            def store(g, j):
                sp.dma_start(att[:, bass.ds((g * GROUP + j) * PAIRED, PAIRED)], AO[:, j % GROUP, :]).then_inc(t.att_stored[j % GROUP], 16)

            def slots(g, first, last):
                for j in range(GROUP):
                    more = not last or j + 1 < GROUP
                    if more:
                        if first and j == 0:
                            sp.wait_ge(sem["kl_ready"], 2)
                        else:
                            sp.wait_ge(sem["att_free"], g * GROUP + j)
                        stack_keys(g, j + 1)
                    if not last or j + 2 < GROUP:
                        load_ct(g, j + 2)
                        load_mask(g, j + 2)
                    if j == 0 and not last:
                        load_ht(g + 1)
                    if more:
                        stack_maxima(g, j + 1)
                        if not first or j:
                            sp.wait_ge(sem["att_ready"], g * GROUP + j)
                            store(g, j - 1)

            load_ht(0)
            for j in range(2):
                load_ct(0, j)
                load_mask(0, j)
            sp.wait_ge(sem["kl_ready"], 1)
            stack_keys(0, 0)
            stack_maxima(0, 0)
            slots(0, True, False)
            with sp.Fori(1, GROUPS - 1) as g:
                slots(g, False, False)
            slots(GROUPS - 1, False, True)
            for j in (GROUP - 2, GROUP - 1):
                sp.wait_ge(sem["att_ready"], (GROUPS - 1) * GROUP + j + 1)
                store(GROUPS - 1, j)
            for j in range(GROUP):
                sp.wait_ge(t.att_stored[j], 16 * GROUPS)

        @block.gpsimd
        def _(pool):
            pl = nc.gpsimd
            pl.memset(QBD[:, HQ:].bitcast(F32), 0.0)
            pl.memset(mx[:, :], 0.0).then_inc(sem["b_cleared"], 1)

            def spread(g, j):
                n = g * GROUP + j
                pool.wait_ge(sem["q_ready"], g + (j // GROUP + 1))
                wait(pool, sem["mx_ready"], n)
                pl.tensor_tensor(QBD[:, 0:HQ].rearrange("p (h q) -> p h q", h=HEADS),
                                 QT[:, ts_(j % GROUP)].unsqueeze(1).to_broadcast([D, HEADS, T]),
                                 t.mask16.unsqueeze(2).to_broadcast([D, HEADS, T]), ALU.mult).then_inc(sem["qbd_ready"], 1)
                wait(pool, sem["pv_done"], (n - 1) * KT)
                for hg in range(HG):
                    last = pl.tensor_tensor(QS[0:96, j % 2, hg * TG:(hg + 1) * TG].rearrange("p (h q) -> p h q", h=HG),
                                            QR[:, hg, ts_(j % GROUP)].bitcast(F32).unsqueeze(1).to_broadcast([96, HG, T]),
                                            K[0:96, K_M4:K_M4 + HG].unsqueeze(2).to_broadcast([96, HG, T]), ALU.mult)
                last.then_inc(sem["qexp_ready"], 1)

            def divide(g, j):
                n = g * GROUP + j
                q = (j - 1) % GROUP
                pool.wait_ge(sem["rd_ready"], n + 1)
                wait(pool, t.att_stored[q], (g + (j - 1) // GROUP) * 16)
                pl.tensor_tensor(AO[:, q, :].rearrange("p (b c t) -> p b c t", b=2, c=2),
                                 OD[:, :].rearrange("p (b c t) -> p b c t", b=2, c=2),
                                 RD[:, :].rearrange("p (b t) -> p b t", b=2).unsqueeze(2).to_broadcast([D, 2, 2, T]),
                                 ALU.mult).then_inc(sem["quotient_ready"], 1)
                pool.wait_ge(sem["quotient_ready"], n)
                both = AO[:, q, :].rearrange("p (b c) -> p b c", b=2)
                bias = t.C[:, CCOL["xv0"]:CCOL["xv0"] + 2].unsqueeze(2).to_broadcast([D, 2, 2 * T])
                pl.tensor_tensor(both, both, bias, ALU.add).then_inc(sem["att_ready"], 1)

            spread(0, 0)
            pl.memset(V[:, :, 0:KT - 1, :, 16:32], 1.0)
            pl.memset(V[:, :, KT - 1, :, :], 0.0).then_inc(sem["v_cleared"], 1)
            pool.wait_ge(sem["v_cleared"], 1)
            pl.memset(V[0:REST, :, KT - 1, :, 16:32], 1.0).then_inc(sem["v_cleared"], 1)
            spread(0, 1)

            def slots(g, first, last):
                for j in range(GROUP):
                    if not first or j:
                        divide(g, j)
                    if not last or j + 2 < GROUP:
                        spread(g, j + 2)

            slots(0, True, False)
            with pool.Fori(1, GROUPS - 1) as g:
                slots(g, False, False)
            slots(GROUPS - 1, False, True)
            divide(GROUPS - 1, GROUP)

        @block.scalar
        def _(act):
            def slots(g, first, last):
                for j in range(GROUP):
                    n = g * GROUP + j
                    for kt in range(KT):
                        for a in range(2):
                            act.wait_ge(sem["st_psum"], n * 2 * KT + (2 * kt + a + 1))
                            if a == 0:
                                wait(act, sem["pv_done"], n * KT + (kt - 1))
                            nc.scalar.activation(PT[:, kt % 2, 2 * a:2 * a + 2, :], psum[:, 2 * a:2 * a + 2, 0:TG],
                                                 ACT.Exp).then_inc(sem["pt_ready"], 1)

            slots(0, True, False)
            with act.Fori(1, GROUPS - 1) as g:
                slots(g, False, False)
            slots(GROUPS - 1, False, True)

        @block.tensor
        def _(pe):
            mm = nc.tensor.matmul
            pe.wait_ge(sem["b_cleared"], 1)

            def job(at, r, g, j, kind, i):
                n = g * GROUP + j
                b = RING[r]
                wait(pe, sem["ring_drained"], at - (len(RING) - 1))
                if kind == "query":
                    if i == 0:
                        pe.wait_ge(sem["ht_loaded"], (g + (j // GROUP + 1)) * 16)
                    if i < 3:
                        c, size = Q_PARTS[i]
                        m = mm(bank(b, D, size), w("xqT"), HT[:, c:c + size], start=True, stop=True)
                    else:
                        c = WSTACK + 96 * (i - 3)
                        m = mm(bank(b, 96, TG), W[:, c:c + 96], HT[:, :], start=True, stop=True)
                elif kind == "key":
                    if i == 0:
                        pe.wait_ge(t.ct_loaded[j % 2], (2 * g + (j // 2 + 1)) * 16)
                    c, size = CHUNKS[i]
                    m = mm(bank(b, D, size), w("xkT"), CT[:, j % 2, c:c + size], start=True, stop=True)
                elif kind == "result":
                    wait(pe, sem["att_free"], n - 1)
                    pairs = OD[:, :].rearrange("p (b c t) -> p b c t", b=2, c=2)
                    for c in range(2):
                        m = mm(bank(b, D, PAIRED // 2).rearrange("p (b t) -> p b t", b=2),
                               K[:, K_SEL + c * D:K_SEL + (c + 1) * D], pairs[:, :, c, :], start=(c == 0), stop=(c == 1))
                elif kind == "value":
                    for k in range(4 * i, 4 * i + 4):
                        rows = D if k < KT - 1 else REST
                        m = mm(bank(b, rows, D, (k % 4) * D), CT[:, j % 2, k * D:k * D + rows], w("xvT"),
                               start=True, stop=True)
                elif kind == "score":
                    q, i = divmod(i, 3)
                    if q == 0 and i == 0:
                        pe.wait_ge(sem["kh_ready"], n + 1)
                        pe.wait_ge(sem["qbd_ready"], n + 1)
                    c, size = CHUNKS[i]
                    m = mm(bank(b, D, size), QBD[:, q * D:(q + 1) * D], KH[:, c:c + size], start=True, stop=True)
                else:
                    pe.wait_ge(sem["mx_ready"], n + 1)
                    m = nc.tensor.transpose(bank(b, QCH, D), mx[:, 0:QCH], t.ident)
                m.then_inc(sem["ring_filled"], 1)

            def score_half(g, j, kt, a):
                n = g * GROUP + j
                if kt == 0 and a == 0:
                    pe.wait_ge(t.ks_loaded[j % 2], (2 * g + (j // 2 + 1)) * 16 * KS_DMAS)
                    pe.wait_ge(t.qrow_loaded[j % 2], (2 * g + (j // 2 + 1)) * 32)
                    pe.wait_ge(sem["qexp_ready"], n + 1)
                wait(pe, sem["pt_ready"], n * 2 * KT + (2 * kt + a - 1))
                for hg in (2 * a, 2 * a + 1):
                    m = mm(bank(hg, D, TG), KS[0:STACK, j % 2, hg, kt * D:(kt + 1) * D],
                           QS[0:STACK, j % 2, hg * TG:(hg + 1) * TG], start=True, stop=True)
                m.then_inc(sem["st_psum"], 1)

            def weigh(g, j, kt, b):
                n = g * GROUP + j
                pe.wait_ge(sem["pt_ready"], n * 2 * KT + (2 * kt + b + 1))
                if kt == 0 and b == 0:
                    wait(pe, sem["att_free"], n)
                for r in range(4):
                    m = mm(psum[32 * r:32 * r + 32, 6, b * 2 * T:(b + 1) * 2 * T], V[:, j % 2, kt, 4 * b + r, :],
                           PT[:, kt % 2, 2 * b + r // 2, (r % 2) * 2 * T:(r % 2 + 1) * 2 * T],
                           start=(kt == 0 and b == 0), stop=(kt == KT - 1), tile_position=(0, 32 * r),
                           skip_group_check=True)
                if b == 1:
                    m.then_inc(sem["pv_done"], 1)

            def slots(g, first, last):
                for j in range(GROUP):
                    jobs = ring_jobs(g, j, last)

                    def some(k):
                        for i, what in enumerate(jobs):
                            if ring_place(jobs, i) == k:
                                job(*bank_number(g, j, i, last), *what)

                    for kt in range(KT):
                        ahead = (j, kt + 1) if kt + 1 < KT else (j + 1, 0)
                        more = not last or ahead[0] < GROUP
                        if more:
                            score_half(g, *ahead, 0)
                        some(4 * kt)
                        if more:
                            score_half(g, *ahead, 1)
                        some(4 * kt + 1)
                        weigh(g, j, kt, 0)
                        some(4 * kt + 2)
                        weigh(g, j, kt, 1)
                        some(4 * kt + 3)

            for i, what in enumerate(first_ring_jobs()):
                job(i, i % len(RING), *what)
            pe.wait_ge(sem["v_cleared"], 2)
            score_half(0, 0, 0, 0)
            score_half(0, 0, 0, 1)
            slots(0, True, False)
            with pe.Fori(1, GROUPS - 1) as g:
                slots(g, False, False)
            slots(GROUPS - 1, False, True)
            job(END, END % len(RING), GROUPS - 1, GROUP + 1, "result", 0)

        @block.vector
        def _(dve):
            v = nc.vector
            link, state = t.linker(dve, sem["b_chain"])
            ts = v.tensor_scalar
            v.memset(OD[:, :], 1.0)
            v.memset(KS[:, :, :, S:].bitcast(F32), 0.0)
            v.memset(QS[96:D, :, :].bitcast(F32), 1.0)
            v.memset(KS[96:D, 0, :, 0:S].bitcast(F32), 1.0)

            def drain(at, r, g, j, kind, i):
                n = g * GROUP + j
                p = j % 2
                b = RING[r]
                drained = sem["ring_drained"]
                dve.wait_ge(sem["ring_filled"], at + 1)
                if kind == "query" and i < 3:
                    if i == 0:
                        wait(dve, sem["qexp_ready"], n)
                    c, size = Q_PARTS[i]
                    ts(QT[:, c:c + size], bank(b, D, size), DK_SCALE, xbq[:, 0:1], ALU.mult, ALU.add)\
                        .then_inc(drained, 1)
                elif kind == "query":
                    hg = i - 3
                    ts(QF[:, :], bank(b, 96, TG), DK_SCALE, xbq[0:96, 2 + hg:3 + hg], ALU.mult, ALU.add)\
                        .then_inc(drained, 1)
                    dve.wait_ge(drained, at + 1)
                    link(v.tensor_copy(QH[:, :], QF[:, :]))
                    m = v.scalar_tensor_tensor(out=QR[:, hg, :], in0=QH[:, :].bitcast(F32), scalar=K[0:96, K_NEG1:K_NEG1 + 1],
                                               in1=QF[:, :], op0=ALU.mult, op1=ALU.add)
                    if hg == HG - 1:
                        m.then_inc(sem["q_ready"], 1)
                        dve.wait_ge(sem["q_ready"], g + (j // GROUP + 1))
                    else:
                        link(m)
                elif kind == "key":
                    if i == 0:
                        dve.wait_ge(t.mask_loaded[p], (2 * g + (j // 2 + 1)) * 16)
                    c, size = CHUNKS[i]
                    v.scalar_tensor_tensor(out=KF[:, c:c + size], in0=bank(b, D, size), scalar=col("xk"),
                                           in1=MB[:, p, c:c + size], op0=ALU.add, op1=ALU.mult).then_inc(drained, 1)
                    if i == 2:
                        dve.wait_ge(drained, at + 1)
                        wait(dve, t.ks_loaded[1 - p], (2 * g + (j - 1) // 2 + 1) * 16 * KS_DMAS)
                        v.tensor_copy(KH[:, :], KF[:, 0:S]).then_inc(sem["kh_ready"], 1)
                        dve.wait_ge(sem["kh_ready"], n + 1)
                        v.tensor_tensor(KL[:, :], KF[:, 0:S], KH[:, :].bitcast(F32), ALU.subtract)\
                            .then_inc(sem["kl_ready"], 1)
                elif kind == "result":
                    wait(dve, sem["att_ready"], n - 2)
                    v.reciprocal(RD[:, :], bank(b, D, PAIRED // 2)).then_inc(drained, 1)
                    dve.wait_ge(drained, at + 1)
                    v.memset(t.carrier[:, :], 0.0).then_inc(sem["rd_ready"], 1)
                elif kind == "value":
                    if i == 0 and isinstance(g, int) and g == 0 and j == 0:
                        dve.wait_ge(sem["v_cleared"], 2)
                    rows_ = V[:, p, :, :, :].rearrange("p k g c -> p (k g) c")
                    if i < 2:
                        v.tensor_copy(rows_[:, 32 * i:32 * i + 32, 0:16],
                                      bank(b).rearrange("p (g c) -> p g c", c=16)).then_inc(drained, 1)
                    else:
                        v.tensor_copy(rows_[:, 64:88, 0:16], bank(b, D, 3 * D).rearrange("p (g c) -> p g c", c=16))
                        v.tensor_copy(rows_[0:REST, 88:96, 0:16],
                                      bank(b, REST, D, 3 * D).rearrange("p (g c) -> p g c", c=16)).then_inc(drained, 1)
                elif kind == "score":
                    q, c = divmod(i, 3)
                    v.tensor_reduce(part_max[:, q, c:c + 1], bank(b, D, CHUNKS[c][1]), AX.X, ALU.max).then_inc(drained, 1)
                    if i == 3 * QCH - 1:
                        dve.wait_ge(drained, at + 1)
                        v.tensor_reduce(mx[:, 0:QCH], part_max[:, :, :], AX.X, ALU.max, negate=True).then_inc(sem["mx_ready"], 1)
                else:
                    wait(dve, t.qrow_loaded[1 - p], (2 * g + (j - 1) // 2 + 1) * 32)
                    link(v.tensor_copy(NMH[:, :], bank(b, QCH, D)))
                    v.tensor_tensor(NML[:, :], bank(b, QCH, D), NMH[:, :].bitcast(F32), ALU.subtract)\
                        .then_inc(sem["nm_ready"], 1)
                    dve.wait_ge(sem["nm_ready"], n + 1)
                    v.memset(t.carrier[:, :], 0.0).then_inc(drained, 1)

            def gather(n):
                dve.wait_ge(sem["pv_done"], n * KT)
                wait(dve, sem["att_ready"], n - 1)
                v.tensor_copy(OD[:, :], bank(6, D, PAIRED)).then_inc(sem["att_free"], 1)

            def slots(g, first, last):
                for j in range(GROUP):
                    if not first or j:
                        gather(g * GROUP + j)
                    for i, what in enumerate(ring_jobs(g, j, last)):
                        drain(*bank_number(g, j, i, last), *what)

            for i, what in enumerate(first_ring_jobs()):
                drain(i, i % len(RING), *what)
                if what[2] == "turn":
                    v.memset(KS[96:D, 1, :, 0:S].bitcast(F32), 1.0)
            first_links = state["n"]
            state["n"], state["base"] = 0, first_links
            slots(0, True, False)
            assert state["n"] == B_LINKS, state["n"]
            with dve.Fori(1, GROUPS - 1) as g:
                state["n"] = 0
                state["base"] = g * B_LINKS + first_links
                slots(g, False, False)
            state["n"] = 0
            state["base"] = (GROUPS - 1) * B_LINKS + first_links
            slots(GROUPS - 1, False, True)
            gather(BATCH)
            drain(END, END % len(RING), GROUPS - 1, GROUP + 1, "result", 0)


def stage_c(nc, t, x1, att, w1, w2, out):
    with ExitStack() as ctx:
        def sb(name, shape, dt=F32):
            return ctx.enter_context(nc.sbuf_tensor("c_" + name, shape, dt))

        sem, psum, K, tanhs, ident = t.sem, t.psum, t.K, t.tanhs, t.ident
        w, col, row, bank, tok_bank = t.w, t.col, t.row, t.bank, t.tok_bank
        XIN = sb("XIN", [T, 2, GROUP, D])
        AIN = sb("AIN", [D, 2, GROUP, PAIRED])
        X = sb("X", [T, 2, GROUP, D])
        H = sb("H", [T, 2, GROUP, D])
        U = sb("U", [T, 2, GROUP, D])
        Y = sb("Y", [T, 2, GROUP, D])
        OUT = sb("OUT", [T, 2, GROUP, D])
        VS = sb("VS", [T, 2, GROUP, HEADS, HD + 1])
        HT = sb("HT", [D, 2, TG])
        FQ = sb("FQ", [D, 2, TG])
        FK = sb("FK", [D, 2, TG])
        KBD = sb("KBD", [D, 2, HQ])
        P = sb("P", [T, 2, HQ])
        PT = sb("PT", [T, 2, 4, TG])
        HE = sb("HE", [D, 2, 2, TG])
        WT = sb("WT", [EXPERTS, 2, TG])
        W1 = sb("W1", [D, FT * D])
        W2 = sb("W2", [D, FT * D])
        dn = sb("dn", [T, 2, 2, HEADS])
        gt = sb("gt", [T, 2, 6, GROUP * EXPERTS])
        gi = sb("gi", [T, 2, GROUP * EXPERTS], U32)
        sm = sb("sm", [T, 2, 2, GROUP])
        stats_ = sb("stats", [T, 2, GROUP, 6])
        mv = sb("mv", [T, 2, GROUP, 2])
        ve = sb("ve", [T, 2, GROUP])
        rs = sb("rs", [T, 2, GROUP])
        half = sb("half", [T, GROUP])

        block = ctx.enter_context(nc.Block())

        @block.sync
        def _(sp):
            def load(i):
                sp.dma_start(AIN[:, :, :, :].rearrange("p h j c -> p (h j c)"),
                             att[:, bass.ds(i * PAIR * PAIRED, PAIR * PAIRED)]).then_inc(sem["c_x_loaded"], 16)
                sp.dma_start(XIN[:, :, :, :].rearrange("p h j d -> p (h j) d"),
                             x1[:, bass.ds(i * PAIR, PAIR), :]).then_inc(sem["c_x_loaded"], 16)

            def pair(i, more):
                if more:
                    sp.wait_ge(sem["c_x_used"], 2 * i + 2)
                    load(i + 1)
                for h in range(2):
                    sp.wait_ge(sem["out_ready"], 2 * i + h + 2)
                    sp.dma_start(out[:, bass.ds((2 * i + h) * GROUP, GROUP), :], OUT[:, h, :, :]).then_inc(sem["out_stored"], 16)

            load(0)
            sp.dma_start(W1[:, :], w1).then_inc(sem["big_loaded"], 16)
            sp.dma_start(W2[:, :], w2).then_inc(sem["big_loaded"], 16)
            with sp.Fori(0, PAIRS - 1) as i:
                pair(i, True)
            pair(PAIRS - 1, False)
            sp.wait_ge(sem["out_stored"], 32 * PAIRS + 1)

        @block.gpsimd
        def _(pool):
            nc.gpsimd.memset(half[:, :], -0.5)
            nc.gpsimd.memset(VS[:, :, :, :, HD:HD + 1], 1.0).then_inc(sem["c_cleared"], 1)
            pool.wait_ge(sem["c_cleared"], 1)
            with pool.Fori(0, PAIRS) as i:
                for k in range(C_NORMS):
                    for h in range(2):
                        pool.wait_ge(sem["c_var_ready"], (i * C_NORMS + k) * 2 + h + 1)
                        nc.gpsimd.tensor_tensor(rs[:, h, :], ve[:, h, :], half[:, :], ALU.pow).then_inc(sem["c_rstd_ready"], 1)

        @block.scalar
        def _(act):
            with act.Fori(0, PAIRS) as i:
                def turned(k, h, **kw):
                    act.wait_ge(sem["c_tok_turned"], (i * C_TURNS + k) * 2 + h + 1)
                    nc.scalar.activation(HT[:, h, :], bank(4 * h, D, TG), **kw).then_inc(sem["c_tokT_ready"], 1)

                for h in range(2):
                    turned(0, h, func=ACT.Copy)
                for h in range(2):
                    act.wait_ge(sem["fqk_psum"], 2 * i + h + 1)
                    nc.scalar.activation(FQ[:, h, :], bank(4 * h + 1, D, TG), ACT.Identity, bias=t.xbq[:, 1:2],
                                         scale=DK_SCALE).then_inc(sem["fq_ready"], 1)
                    nc.scalar.activation(FK[:, h, :], bank(4 * h + 2, D, TG), ACT.Identity,
                                         bias=col("fk")).then_inc(sem["fk_ready"], 1)
                    act.wait_ge(sem["fv_psum"], 2 * i + h + 1)
                    nc.scalar.copy(VS[:, h, :, :, :].rearrange("p j a d -> p (j a) d")[:, :, 0:HD],
                                   bank(4 * h + 3, T).rearrange("p (a d) -> p a d", d=HD)).then_inc(sem["fv_ready"], 1)

                def probabilities(m):
                    act.wait_ge(sem["fsub_ready"], i * PAIR + m + 1)
                    nc.scalar.activation(P[:, m % 2, :], P[:, m % 2, :], ACT.Exp).then_inc(sem["fe_ready"], 1)

                probabilities(0)
                for m in range(PAIR):
                    n = i * PAIR + m
                    for c in range(2):
                        act.wait_ge(sem["feT_psum"], 2 * n + c + 1)
                        if c == 0 and m >= 2:
                            act.wait_ge(sem["fo_psum"], n - 1)
                        b = 4 * (m % 2) + 2 * c
                        nc.scalar.copy(PT[:, m % 2, 2 * c:2 * c + 2, :], psum[0:T, b:b + 2, 0:TG]).then_inc(sem["feT_ready"], 1)
                    if m + 1 < PAIR:
                        probabilities(m + 1)
                for h in range(2):
                    turned(1, h, func=ACT.Identity, bias=col("fv"))
                for h in range(2):
                    turned(2, h, func=ACT.Copy)

                def relu(u):
                    h, e = divmod(u, EXPERTS)
                    for f in range(2):
                        act.wait_ge(sem["moe_h_psum"], (i * 2 * EXPERTS + u) * 2 + f + 1)
                        if f == 0 and u >= 2:
                            act.wait_ge(sem["moe_y_psum"], i * 2 * EXPERTS + u - 1)
                        c = CB1 + 2 * e + f
                        nc.scalar.activation(HE[:, u % 2, f, :], bank(HB[(2 * u + f) % 4], D, TG), ACT.Relu,
                                             bias=t.C[:, c:c + 1]).then_inc(sem["moe_h_ready"], 1)

                relu(0)
                relu(1)
                for h in range(2):
                    act.wait_ge(sem["gsub_ready"], 2 * i + h + 1)
                    nc.scalar.activation(gt[:, h, 1, :], gt[:, h, 1, :], ACT.Exp).then_inc(sem["gexp_ready"], 1)
                for h in range(2):
                    act.wait_ge(sem["wT_psum"], 2 * i + h + 1)
                    nc.scalar.copy(WT[:, h, :], bank(4 * h + 3, EXPERTS, TG)).then_inc(sem["wT_ready"], 1)
                for u in range(2, 2 * EXPERTS):
                    relu(u)

        @block.tensor
        def _(pe):
            mm = nc.tensor.matmul
            with pe.Fori(0, PAIRS) as i:
                def turn(k, src):
                    for h in range(2):
                        pe.wait_ge(sem["c_tok_ready"], (i * C_TURNS + k) * 2 + h + 1)
                        for j in range(GROUP):
                            m = nc.tensor.transpose(bank(4 * h, D, T, j * T), src[:, h, j, :], ident[0:T, 0:T])
                        m.then_inc(sem["c_tok_turned"], 1)

                def wait_turned(k, h):
                    pe.wait_ge(sem["c_tokT_ready"], (i * C_TURNS + k) * 2 + h + 1)

                def per_seq(b, lhsT, rhs, sig, width=D):
                    for j in range(GROUP):
                        m = mm(bank(b, T, width, j * width), lhsT[:, t.ts_(j)], rhs, start=True, stop=True)
                    m.then_inc(sem[sig], 1)

                pe.wait_ge(sem["c_x_loaded"], 32 * (i + 1))
                pe.wait_ge(sem["out_ready"], 2 * i + 1)
                for h in range(2):
                    for j in range(GROUP):
                        for c in range(4):
                            m = mm(bank(4 * h, T, D, j * D), AIN[:, h, j, t.ts_(c)], w(f"xo{c}"), start=(c == 0), stop=(c == 3))
                    m.then_inc(sem["attx_psum"], 1)
                turn(0, H)
                for h in range(2):
                    wait_turned(0, h)
                    mm(bank(4 * h + 1, D, TG), w("fq"), HT[:, h, :], start=True, stop=True)
                    mm(bank(4 * h + 2, D, TG), w("fk"), HT[:, h, :], start=True, stop=True).then_inc(sem["fqk_psum"], 1)
                    per_seq(4 * h + 3, HT[:, h, :], w("fv"), "fv_psum")

                def scores(m):
                    h, j = divmod(m, GROUP)
                    if m < 2:
                        pe.wait_ge(sem["fk_ready"], 2 * i + m + 1)
                        pe.wait_ge(sem["fv_ready"], 2 * i + m + 1)
                    else:
                        pe.wait_ge(sem["fu_ready"], i * PAIR + m - 1)
                    pe.wait_ge(sem["kbd_ready"], i * PAIR + m + 1)
                    for c in range(4):
                        x_ = mm(bank(4 * (m % 2) + c, T, TG), FQ[:, h, t.ts_(j)], KBD[:, m % 2, c * TG:(c + 1) * TG],
                                start=True, stop=True)
                    x_.then_inc(sem["fs_psum"], 1)

                scores(0)
                scores(1)
                for m in range(PAIR):
                    h, j = divmod(m, GROUP)
                    n = i * PAIR + m
                    pe.wait_ge(sem["fe_ready"], n + 1)
                    for a in range(HEADS):
                        x_ = nc.tensor.transpose(bank(4 * (m % 2) + a // 4, T, T, (a % 4) * T),
                                                 P[:, m % 2, a * T:(a + 1) * T], ident[0:T, 0:T])
                        if a % 8 == 7:
                            x_.then_inc(sem["feT_psum"], 1)
                    for a in range(HEADS):
                        if a % 8 == 0:
                            pe.wait_ge(sem["feT_ready"], 2 * n + a // 8 + 1)
                        x_ = mm(bank(4 * (m % 2), T, HD + 1, a * (HD + 1)), PT[:, m % 2, a // 4, t.ts_(a % 4)],
                                VS[:, h, j, a, :], start=True, stop=True)
                    x_.then_inc(sem["fo_psum"], 1)
                    if m + 2 < PAIR:
                        scores(m + 2)
                turn(1, U)
                for h in range(2):
                    wait_turned(1, h)
                    per_seq(4 * h + 1, HT[:, h, :], w("fo"), "wo_psum")
                turn(2, Y)
                for h in range(2):
                    wait_turned(2, h)
                    per_seq(4 * h + 2, HT[:, h, :], t.W[:, WGATE:WGATE + EXPERTS], "gate_psum", EXPERTS)

                def hidden(u):
                    h, e = divmod(u, EXPERTS)
                    for f in range(2):
                        n = 2 * e + f
                        if u >= 2:
                            pe.wait_ge(sem["moe_h_ready"], (i * 2 * EXPERTS + u) * 2 + f - 3)
                        mm(bank(HB[(2 * u + f) % 4], D, TG), W1[:, n * D:(n + 1) * D], HT[:, h, :],
                           start=True, stop=True).then_inc(sem["moe_h_psum"], 1)

                pe.wait_ge(sem["big_loaded"], 32)
                hidden(0)
                hidden(1)
                for h in range(2):
                    pe.wait_ge(sem["w_ready"], 2 * i + h + 1)
                    for j in range(GROUP):
                        x_ = nc.tensor.transpose(bank(4 * h + 3, EXPERTS, T, j * T),
                                                 gt[:, h, 2, j * EXPERTS:(j + 1) * EXPERTS], ident[0:T, 0:T])
                    x_.then_inc(sem["wT_psum"], 1)
                for h in range(2):
                    pe.wait_ge(sem["wT_ready"], 2 * i + h + 1)
                    per_seq(4 * h + 2, WT[:, h, :], t.B2[:, :], "b2_psum")
                for u in range(2 * EXPERTS):
                    h, e = divmod(u, EXPERTS)
                    pe.wait_ge(sem["moe_h_ready"], (i * 2 * EXPERTS + u) * 2 + 2)
                    if u >= 2:
                        pe.wait_ge(sem["moe_y_used"], i * 2 * EXPERTS + u - 1)
                    for j in range(GROUP):
                        for f in range(2):
                            n = 2 * e + f
                            x_ = mm(bank(3 + 4 * (u % 2), T, D, j * D), HE[:, u % 2, f, t.ts_(j)], W2[:, n * D:(n + 1) * D],
                                    start=(f == 0), stop=(f == 1))
                    x_.then_inc(sem["moe_y_psum"], 1)
                    if u + 2 < 2 * EXPERTS:
                        hidden(u + 2)

        @block.vector
        def _(dve):
            v = nc.vector
            link, state = t.linker(dve, sem["c_chain"])
            ts = v.tensor_scalar
            dve.wait_ge(sem["c_cleared"], 1)
            v.memset(t.carrier[:, :], 0.0).then_inc(sem["out_stored"], 1)
            dve.wait_ge(sem["out_stored"], 1)
            v.memset(t.carrier[:, :], 0.0).then_inc(sem["out_ready"], 1)
            dve.wait_ge(sem["out_ready"], 1)
            with dve.Fori(0, PAIRS) as i:
                state["n"] = 0
                state["base"] = i * C_LINKS

                def tok_done(ins, k, h):
                    ins.then_inc(sem["c_tok_ready"], 1)
                    dve.wait_ge(sem["c_tok_ready"], (i * C_TURNS + k) * 2 + h + 1)

                def moments(h, src):
                    for j in range(GROUP):
                        last = v.bn_stats(stats_[:, h, j, :], src[:, h, j, :])
                    link(last, plain=True)
                    for j in range(GROUP):
                        last = v.bn_aggr(mv[:, h, j, :], stats_[:, h, j, :])
                    link(last)
                    ts(ve[:, h, :], mv[:, h, :, 1], EPS, None, ALU.add).then_inc(sem["c_var_ready"], 1)

                def normed(k, h, src, dst, gain=None):
                    dve.wait_ge(sem["c_rstd_ready"], (i * C_NORMS + k) * 2 + h + 1)
                    for j in range(GROUP):
                        last = ts(dst[:, h, j, :], src[:, h, j, :], mv[:, h, j, 0:1], rs[:, h, j:j + 1],
                                  ALU.subtract, ALU.mult)
                    if gain is None:
                        return last
                    link(last)
                    link(v.tensor_tensor(dst[:, h, :, :], dst[:, h, :, :], row(gain + "g"), ALU.mult))
                    return v.tensor_tensor(dst[:, h, :, :], dst[:, h, :, :], row(gain + "b"), ALU.add)

                dve.wait_ge(sem["c_x_loaded"], 32 * (i + 1))
                for h in range(2):
                    dve.wait_ge(sem["attx_psum"], 2 * i + h + 1)
                    link(v.tensor_tensor(U[:, h, :, :], tok_bank(4 * h), row("xbo"), ALU.add))
                    v.scalar_tensor_tensor(out=X[:, h, :, :], in0=U[:, h, :, :], scalar=tanhs[:, 1:2], in1=XIN[:, h, :, :],
                                           op0=ALU.mult, op1=ALU.add).then_inc(sem["c_x_used"], 1)
                    dve.wait_ge(sem["c_x_used"], 2 * i + h + 1)
                    moments(h, X)
                for h in range(2):
                    tok_done(normed(0, h, X, H), 0, h)

                def spread(m):
                    h, j = divmod(m, GROUP)
                    if m >= 2:
                        dve.wait_ge(sem["fs_psum"], i * PAIR + m - 1)
                    v.tensor_tensor(KBD[:, m % 2, :].rearrange("p (h k) -> p h k", h=HEADS),
                                    FK[:, h, t.ts_(j)].unsqueeze(1).to_broadcast([D, HEADS, T]),
                                    t.mask16.unsqueeze(2).to_broadcast([D, HEADS, T]), ALU.mult).then_inc(sem["kbd_ready"], 1)

                def divide(m):
                    h, j = divmod(m, GROUP)
                    dve.wait_ge(sem["fo_psum"], i * PAIR + m + 1)
                    fo = psum[0:T, 4 * (m % 2), 0:HEADS * (HD + 1)].rearrange("p (h d) -> p h d", h=HEADS)
                    link(v.reciprocal(dn[:, m % 2, 1, :], fo[:, :, HD]))
                    v.tensor_tensor(U[:, h, j, :].rearrange("p (h d) -> p h d", h=HEADS), fo[:, :, 0:HD],
                                    dn[:, m % 2, 1, :].unsqueeze(2).to_broadcast([T, HEADS, HD]), ALU.mult)\
                        .then_inc(sem["fu_ready"], 1)

                dve.wait_ge(sem["fk_ready"], 2 * i + 1)
                spread(0)
                spread(1)
                for m in range(PAIR):
                    n = i * PAIR + m
                    dve.wait_ge(sem["fs_psum"], n + 1)
                    sc = psum[0:T, 4 * (m % 2):4 * (m % 2) + 4, 0:TG].rearrange("p b (h k) -> p b h k", h=4)
                    link(v.tensor_reduce(dn[:, m % 2, 0, :], sc, AX.X, ALU.max))
                    for c in range(4):
                        last = v.tensor_tensor(P[:, m % 2, c * TG:(c + 1) * TG].rearrange("p (h k) -> p h k", h=4),
                                               sc[:, c, :, :],
                                               dn[:, m % 2, 0, 4 * c:4 * c + 4].unsqueeze(2).to_broadcast([T, 4, T]),
                                               ALU.subtract)
                    last.then_inc(sem["fsub_ready"], 1)
                    if m:
                        divide(m - 1)
                    if m + 2 < PAIR:
                        if m + 2 == GROUP:
                            dve.wait_ge(sem["fk_ready"], 2 * i + 2)
                        spread(m + 2)
                divide(PAIR - 1)
                dve.wait_ge(sem["fu_ready"], (i + 1) * PAIR)
                for h in range(2):
                    tok_done(v.memset(t.carrier[:, :], 0.0), 1, h)
                for h in range(2):
                    dve.wait_ge(sem["wo_psum"], 2 * i + h + 1)
                    link(v.tensor_tensor(U[:, h, :, :], tok_bank(4 * h + 1), row("fbo"), ALU.add))
                    link(v.tensor_tensor(U[:, h, :, :], U[:, h, :, :], H[:, h, :, :], ALU.add))
                    moments(h, U)
                for h in range(2):
                    tok_done(normed(1, h, U, Y, "fln1"), 2, h)
                wide = [T, GROUP, EXPERTS]

                def ge(h, a):
                    return gt[:, h, a, :].rearrange("p (j e) -> p j e", j=GROUP)

                def gj(h, a, j):
                    return gt[:, h, a, j * EXPERTS:(j + 1) * EXPERTS]
                for h in range(2):
                    dve.wait_ge(sem["gate_psum"], 2 * i + h + 1)
                    link(v.tensor_tensor(ge(h, 0), psum[0:T, 4 * h + 2, 0:GROUP * EXPERTS].rearrange("p (j e) -> p j e", j=GROUP),
                                         t.R[:, RGB:RGB + EXPERTS].unsqueeze(1).to_broadcast(wide), ALU.add))
                    link(v.tensor_reduce(sm[:, h, 0, :], ge(h, 0), AX.X, ALU.max))
                    v.tensor_tensor(ge(h, 1), ge(h, 0), sm[:, h, 0, :].unsqueeze(2).to_broadcast(wide), ALU.subtract)\
                        .then_inc(sem["gsub_ready"], 1)
                for h in range(2):
                    dve.wait_ge(sem["gexp_ready"], 2 * i + h + 1)
                    link(v.tensor_reduce(sm[:, h, 1, :], ge(h, 1), AX.X, ALU.add))
                    link(v.reciprocal(sm[:, h, 1, :], sm[:, h, 1, :]))
                    link(v.tensor_tensor(ge(h, 0), ge(h, 1), sm[:, h, 1, :].unsqueeze(2).to_broadcast(wide), ALU.mult), plain=True)
                    for j in range(GROUP):
                        last = v.max(gj(h, 3, j), gj(h, 0, j))
                    link(last, plain=True)
                    for j in range(GROUP):
                        last = v.max_index(gi[:, h, j * EXPERTS:(j + 1) * EXPERTS], gj(h, 3, j), gj(h, 0, j))
                    link(last)
                    link(v.tensor_copy(gt[:, h, 4, :], gi[:, h, :]))
                    iota8 = K[0:T, K_IOTA:K_IOTA + EXPERTS]
                    for j in range(GROUP):
                        for n, dst in ((0, 2), (1, 5)):
                            last = ts(gj(h, dst, j), iota8, gj(h, 4, j)[:, n:n + 1], gj(h, 3, j)[:, n:n + 1],
                                      ALU.is_equal, ALU.mult)
                    link(last)
                    v.tensor_tensor(gt[:, h, 2, :], gt[:, h, 2, :], gt[:, h, 5, :], ALU.add).then_inc(sem["w_ready"], 1)
                    dve.wait_ge(sem["w_ready"], 2 * i + h + 1)
                for h in range(2):
                    dve.wait_ge(sem["b2_psum"], 2 * i + h + 1)
                    link(v.tensor_tensor(U[:, h, :, :], tok_bank(4 * h + 2), Y[:, h, :, :], ALU.add))

                def finish(h):
                    link(normed(2, h, U, H, "fln2"))
                    if h == 0:
                        dve.wait_ge(sem["out_stored"], 32 * i + 1)
                    v.scalar_tensor_tensor(out=OUT[:, h, :, :], in0=H[:, h, :, :], scalar=tanhs[:, 3:4], in1=X[:, h, :, :],
                                           op0=ALU.mult, op1=ALU.add).then_inc(sem["out_ready"], 1)

                for u in range(2 * EXPERTS):
                    h, e = divmod(u, EXPERTS)
                    dve.wait_ge(sem["moe_y_psum"], i * 2 * EXPERTS + u + 1)
                    for j in range(GROUP):
                        last = v.scalar_tensor_tensor(out=U[:, h, j, :], in0=tok_bank(3 + 4 * (u % 2))[:, j, :],
                                                      scalar=gj(h, 2, j)[:, e:e + 1], in1=U[:, h, j, :],
                                                      op0=ALU.mult, op1=ALU.add)
                    last.then_inc(sem["moe_y_used"], 1)
                    dve.wait_ge(sem["moe_y_used"], i * 2 * EXPERTS + u + 1)
                    if u == EXPERTS:
                        moments(0, U)
                    if u == EXPERTS + 1:
                        finish(0)
                moments(1, U)
                finish(1)
                dve.wait_ge(sem["out_ready"], 2 * i + 3)
                assert state["n"] == C_LINKS, state["n"]


def kernel(**inputs):
    import numpy as np
    import concourse.bacc as bacc
    from concourse.bass_utils import run_bass_kernel_spmd

    a = {n: np.asarray(v) for n, v in inputs.items()}
    f = np.float32

    weights = {
        "q1T": a["L0_xattn_Wq1"].T, "k1T": a["L0_xattn_Wk1"].T, "q2T": a["L0_xattn_Wq2"].T, "k2T": a["L0_xattn_Wk2"].T,
        "v1": a["L0_xattn_Wv1"], "v2": a["L0_xattn_Wv2"], "fc1": a["L0_xattn_fc1_w"], "fc2": a["L0_xattn_fc2_w"],
        "xqT": a["L1_xattn_Wq"].T, "xkT": a["L1_xattn_Wk"].T, "xvT": a["L1_xattn_Wv"].T,
        "fq": a["L1_ffn_Wq"], "fk": a["L1_ffn_Wk"], "fv": a["L1_ffn_Wv"], "fo": a["L1_ffn_Wo"],
    }
    wo = a["L1_xattn_Wo"].T.reshape(2, 4, 2, HD, D)
    paired_bv = a["L1_xattn_bv"].reshape(2, 4, 2, HD)
    bv = np.zeros((2, 4, 4, HD), f)
    bv[:, :, 0:2] = paired_bv
    for b in range(2):
        for c in range(2):
            rows_ = np.zeros((4, 4, HD, D), f)
            rows_[:, c] = wo[b, :, c]
            weights[f"xo{2 * b + c}"] = rows_.reshape(D, D)
    stacks = [np.tile(a["L1_xattn_Wq"].T[:, 32 * g:32 * g + 32], (1, 3)) for g in range(4)]
    wpack = np.concatenate([weights[n] for n in WNAMES] + stacks + [a["L1_ffn_gW"]], axis=1)
    cols = {"fc1": a["L0_xattn_fc1_b"], "xq": a["L1_xattn_bq"], "xk": a["L1_xattn_bk"], "xv0": bv[0].reshape(D), "xv1": bv[1].reshape(D),
            "fq": a["L1_ffn_bq"], "fk": a["L1_ffn_bk"], "fv": a["L1_ffn_bv"]}
    pad = np.zeros(32, f)
    bq = [np.concatenate([np.tile(a["L1_xattn_bq"][32 * g:32 * g + 32], 3), pad]) for g in range(4)]
    cpack = np.stack([cols[n] for n in CNAMES] + list(a["L1_ffn_b1"].reshape(FT, D)) + bq, axis=1)
    rows = {"ln1g": a["L0_xattn_ln1_g"], "ln1b": a["L0_xattn_ln1_b"], "ln2g": a["L0_xattn_ln2_g"], "ln2b": a["L0_xattn_ln2_b"],
            "ln3g": a["L0_xattn_ln3_g"], "ln3b": a["L0_xattn_ln3_b"], "fc2b": a["L0_xattn_fc2_b"], "xbo": a["L1_xattn_bo"],
            "fbo": a["L1_ffn_bo"], "fln1g": a["L1_ffn_ln1_g"], "fln1b": a["L1_ffn_ln1_b"],
            "fln2g": a["L1_ffn_ln2_g"], "fln2b": a["L1_ffn_ln2_b"]}
    rpack = np.concatenate([rows[n] for n in RNAMES] + [a["L1_ffn_gb"], a["g_xattn"], a["g_ffn"]])
    kpack = np.zeros((D, KPACK), f)
    p = np.arange(D)
    kpack[:, K_ID:K_ID + D] = np.eye(D)
    kpack[:, K_M16:K_M16 + HEADS] = p[:, None] // HD == np.arange(HEADS)[None]
    kpack[:, K_M4:K_M4 + HG] = p[:, None] // HD % HG == np.arange(HG)[None]
    kpack[32:64, K_NEG1] = -1.0
    t = np.arange(T)
    kpack[:T, K_BASE:K_BASE + T] = np.where(t[None] <= t[:, None], -(t[None] + 0.5), -1e6)
    for c in range(2):
        here = (p // HD % 4 == 1) if c else (p // HD % 4 != 1)
        kpack[:, K_SEL + c * D:K_SEL + (c + 1) * D] = (p[:, None] % 32 == 16) & (p[:, None] // 32 == p[None] // 32) & here[None]
    kpack[:, K_IOTA:K_IOTA + EXPERTS] = np.arange(EXPERTS)
    arrays = {
        "x": a["x"].transpose(1, 0, 2), "ctxn": a["ctx_1024"], "ctxt": a["ctx_1024"].transpose(0, 2, 1),
        "mask": a["mask_BxS2_bf1"].view(np.uint8), "wpack": wpack, "cpack": cpack, "rpack": rpack, "kpack": kpack,
        "w1": a["L1_ffn_W1"].transpose(1, 0, 2).reshape(D, FT * D),
        "w2": a["L1_ffn_W2"].reshape(FT, D, D).transpose(1, 0, 2).reshape(D, FT * D),
        "b2": a["L1_ffn_b2"],
        "wgu": np.concatenate([a["L0_ffn_w_gate"].T, a["L0_ffn_w_up"].T,
                               a["L0_ffn_w_down"].T.reshape(4, D, D).transpose(1, 0, 2).reshape(D, 4 * D)], axis=1),
    }
    nc = bacc.Bacc("TRN2", target_bir_lowering=False, num_devices=1)
    feeds, args = {}, []
    for name, value in arrays.items():
        value = np.ascontiguousarray(value)
        feeds[f"in_{name}"] = value
        args.append(nc.dram_tensor(f"in_{name}", value.shape, mybir.dt.from_np(value.dtype), kind="ExternalInput").ap())
    out = nc.dram_tensor("out_tokens", [T, BATCH, D], F32, kind="ExternalOutput").ap()
    build(nc, *args, out)
    r = run_bass_kernel_spmd(nc, [feeds], core_ids=[0])
    return np.ascontiguousarray(r.results[0]["out_tokens"].transpose(1, 0, 2))
```
